# Optimizing a Trainium2 kernel written in Bass

```python
import numpy as np
import jax
import jax.numpy as jnp

def _softmax(x, axis=-1):
    return jax.nn.softmax(x, axis=axis)

def _gelu(x):
    return jax.nn.gelu(x, approximate=True)

def _silu(x):
    return jax.nn.silu(x)

def _sigmoid(x):
    return jax.nn.sigmoid(x)

def _layernorm(x, axis=-1, eps=1e-05):
    m = jnp.mean(x, axis=axis, keepdims=True)
    v = jnp.var(x, axis=axis, keepdims=True)
    return (x - m) / jnp.sqrt(v + eps)

def _scatter_add(tgt, idx, src, axis=0):
    return tgt.at[idx].add(src)

def _segment_sum(src, seg, n):
    return jax.ops.segment_sum(src, seg, n)
kernel_name = 'mk_gnn_preln_d4_gnn_r64_3c44a3'

def setup_inputs(seed: int=0):
    np.random.seed(seed)
    _w = jnp.asarray

    def _rec_inputs():
        import jax
        import jax.numpy as jnp
        _gk = jax.random.key(seed)
        x = -0.0005121 + 1.001 * jax.random.normal(jax.random.fold_in(_gk, 1), (100000, 64), jnp.float32)
        src = jax.random.randint(jax.random.fold_in(_gk, 2), (50000,), 0, 100000, jnp.int32)
        dst = jnp.minimum((100000 * jax.random.uniform(jax.random.fold_in(_gk, 3), (50000,)) ** 2.0).astype(jnp.int32), 99999)
        _o = jnp.argsort(dst, stable=True)
        src = src[_o]
        dst = dst[_o]
        edge_type_8 = jax.random.randint(jax.random.fold_in(_gk, 13), (50000,), 0, 8, jnp.int32)
        return (x, src, dst, edge_type_8)
    x, src, dst, edge_type_8 = _rec_inputs()

    def _L0_gnn_setup():
        import jax, jax.numpy as jnp
        import numpy as np
        N_NODES = 50000
        N_EDGES = 12500
        D_IN = 64
        D_OUT = 64
        key = jax.random.key(seed)
        k1, k2, k3, k4 = jax.random.split(key, 4)
        x = jax.random.normal(k1, (N_NODES, D_IN), dtype=jnp.float32)
        edge_index = jax.random.randint(k2, (2, N_EDGES), 0, N_NODES, dtype=jnp.int64)
        lim = 1.0 / np.sqrt(D_IN)
        W = jax.random.uniform(k3, (D_OUT, D_IN), dtype=jnp.float32, minval=-lim, maxval=lim)
        b = jax.random.uniform(k4, (D_OUT,), dtype=jnp.float32, minval=-lim, maxval=lim)
        return {'x': x, 'edge_index': edge_index, 'W': W, 'b': b}
    _L0_gnn_all = _L0_gnn_setup()
    _L0_gnn_in = {k: v for k, v in _L0_gnn_all.items() if k in ('W', 'b')}
    del _L0_gnn_all

    def _L1_gnn_setup():
        import jax, jax.numpy as jnp
        import numpy as np
        N_NODES = 100000
        N_EDGES = 20000
        HID = 64
        MSG = 64
        N_ETYPE = 8

        def _ggnn_forward(h, edge_matrix, w_ih, w_hh, b_ih, b_hh, edge_src, edge_dst, edge_type):
            N, H = h.shape
            T = edge_matrix.shape[0]
            M = edge_matrix.shape[1] // H
            A = edge_matrix.reshape(T, M, H)
            Ht = jnp.einsum('tmh,nh->tnm', A, h)
            msg = Ht[edge_type, edge_src]
            m_agg = jax.ops.segment_sum(msg, edge_dst, num_segments=N)
            gi = m_agg @ w_ih.T + b_ih
            gh = h @ w_hh.T + b_hh
            i_r, i_z, i_n = (gi[:, :H], gi[:, H:2 * H], gi[:, 2 * H:])
            h_r, h_z, h_n = (gh[:, :H], gh[:, H:2 * H], gh[:, 2 * H:])
            r = jax.nn.sigmoid(i_r + h_r)
            z = jax.nn.sigmoid(i_z + h_z)
            n = jnp.tanh(i_n + r * h_n)
            return (1.0 - z) * n + z * h
        key = jax.random.key(seed)
        ks = jax.random.split(key, 9)
        s = 1.0 / np.sqrt(HID)
        return {'h': jax.random.normal(ks[0], (N_NODES, HID), jnp.float32) * s, 'edge_matrix': jax.random.normal(ks[1], (N_ETYPE, MSG * HID), jnp.float32) * s, 'w_ih': jax.random.normal(ks[2], (3 * HID, MSG), jnp.float32) * s, 'w_hh': jax.random.normal(ks[3], (3 * HID, HID), jnp.float32) * s, 'b_ih': jax.random.normal(ks[4], (3 * HID,), jnp.float32) * s, 'b_hh': jax.random.normal(ks[5], (3 * HID,), jnp.float32) * s, 'edge_src': jax.random.randint(ks[6], (N_EDGES,), 0, N_NODES, jnp.int32), 'edge_dst': jax.random.randint(ks[7], (N_EDGES,), 0, N_NODES, jnp.int32), 'edge_type': jax.random.randint(ks[8], (N_ETYPE if False else N_EDGES,), 0, N_ETYPE, jnp.int32)}
    _L1_gnn_all = _L1_gnn_setup()
    _L1_gnn_in = {k: v for k, v in _L1_gnn_all.items() if k in ('edge_matrix', 'w_ih', 'w_hh', 'b_ih', 'b_hh')}
    del _L1_gnn_all

    def _L2_gnn_setup():
        import jax, jax.numpy as jnp
        import numpy as np
        N, E, H, D = (50000, 12500, 4, 64)
        IN = D
        EPS = 1e-05
        key = jax.random.key(seed)
        ks = jax.random.split(key, 9)
        s = 1.0 / np.sqrt(IN)
        return {'h': jax.random.normal(ks[0], (N, IN), dtype=jnp.float32), 'src': jax.random.randint(ks[1], (E,), 0, N), 'dst': jax.random.randint(ks[2], (E,), 0, N), 'Wq': jax.random.uniform(ks[3], (IN, H * D), jnp.float32, -s, s), 'Wk': jax.random.uniform(ks[4], (IN, H * D), jnp.float32, -s, s), 'Wv': jax.random.uniform(ks[5], (IN, H * D), jnp.float32, -s, s), 'Wo': jax.random.uniform(ks[6], (H * D, D), jnp.float32, -1.0 / np.sqrt(H * D), 1.0 / np.sqrt(H * D)), 'gamma': jnp.ones((D,), jnp.float32), 'beta': jnp.zeros((D,), jnp.float32)}
    _L2_gnn_all = _L2_gnn_setup()
    _L2_gnn_in = {k: v for k, v in _L2_gnn_all.items() if k in ('Wq', 'Wk', 'Wv', 'Wo', 'gamma', 'beta')}
    del _L2_gnn_all

    def _L3_gnn_setup():
        import jax, jax.numpy as jnp
        import numpy as np
        N_NODES = 100000
        N_EDGES = 25000
        D_IN = 64
        D_OUT = 64
        LEAKY_SLOPE = 0.01
        key = jax.random.key(seed)
        k1, k2, k3, k4, k5 = jax.random.split(key, 5)
        feat = jax.random.normal(k1, (N_NODES, D_IN), dtype=jnp.float32)
        scale = jnp.sqrt(2.0 / (D_IN + D_OUT)).astype(jnp.float32)
        W1 = jax.random.normal(k2, (D_IN, D_OUT), dtype=jnp.float32) * scale
        W2 = jax.random.normal(k3, (D_IN, D_OUT), dtype=jnp.float32) * scale
        src = jax.random.randint(k4, (N_EDGES,), 0, N_NODES, dtype=jnp.int64 if jax.config.jax_enable_x64 else jnp.int32)
        dst = jax.random.randint(k5, (N_EDGES,), 0, N_NODES, dtype=jnp.int64 if jax.config.jax_enable_x64 else jnp.int32)
        return {'feat': feat, 'W1': W1, 'W2': W2, 'src': src, 'dst': dst}
    _L3_gnn_all = _L3_gnn_setup()
    _L3_gnn_in = {k: v for k, v in _L3_gnn_all.items() if k in ('W1', 'W2')}
    del _L3_gnn_all
    return {'x': x, 'src': src, 'dst': dst, 'edge_type_8': edge_type_8, 'L0_gnn_W': _L0_gnn_in['W'], 'L0_gnn_b': _L0_gnn_in['b'], 'L1_gnn_edge_matrix': _L1_gnn_in['edge_matrix'], 'L1_gnn_w_ih': _L1_gnn_in['w_ih'], 'L1_gnn_w_hh': _L1_gnn_in['w_hh'], 'L1_gnn_b_ih': _L1_gnn_in['b_ih'], 'L1_gnn_b_hh': _L1_gnn_in['b_hh'], 'L2_gnn_Wq': _L2_gnn_in['Wq'], 'L2_gnn_Wk': _L2_gnn_in['Wk'], 'L2_gnn_Wv': _L2_gnn_in['Wv'], 'L2_gnn_Wo': _L2_gnn_in['Wo'], 'L2_gnn_gamma': _L2_gnn_in['gamma'], 'L2_gnn_beta': _L2_gnn_in['beta'], 'L3_gnn_W1': _L3_gnn_in['W1'], 'L3_gnn_W2': _L3_gnn_in['W2']}

def reference(x, src, dst, edge_type_8, L0_gnn_W, L0_gnn_b, L1_gnn_edge_matrix, L1_gnn_w_ih, L1_gnn_w_hh, L1_gnn_b_ih, L1_gnn_b_hh, L2_gnn_Wq, L2_gnn_Wk, L2_gnn_Wv, L2_gnn_Wo, L2_gnn_gamma, L2_gnn_beta, L3_gnn_W1, L3_gnn_W2):
    import jax
    import jax.numpy as jnp

    def _L0_gnn_ref(x, edge_index, W, b):
        import jax, jax.numpy as jnp
        import numpy as np
        N_NODES = 50000
        N_EDGES = 12500
        D_IN = 64
        D_OUT = 64
        N = x.shape[0]
        loops = jnp.arange(N, dtype=edge_index.dtype)
        ei = jnp.concatenate([edge_index, jnp.stack([loops, loops], axis=0)], axis=1)
        row, col = (ei[0], ei[1])
        h = x @ W.T + b
        deg = jax.ops.segment_sum(jnp.ones(row.shape, dtype=h.dtype), row, num_segments=N)
        dinv = deg ** (-0.5)
        norm = dinv[row] * dinv[col]
        msg = norm[:, None] * h[col]
        return jax.ops.segment_sum(msg, row, num_segments=N)

    def _L1_gnn_ref(h, edge_matrix, w_ih, w_hh, b_ih, b_hh, edge_src, edge_dst, edge_type):
        import jax, jax.numpy as jnp
        import numpy as np
        N_NODES = 100000
        N_EDGES = 20000
        HID = 64
        MSG = 64
        N_ETYPE = 8

        def _ggnn_forward(h, edge_matrix, w_ih, w_hh, b_ih, b_hh, edge_src, edge_dst, edge_type):
            N, H = h.shape
            T = edge_matrix.shape[0]
            M = edge_matrix.shape[1] // H
            A = edge_matrix.reshape(T, M, H)
            Ht = jnp.einsum('tmh,nh->tnm', A, h)
            msg = Ht[edge_type, edge_src]
            m_agg = jax.ops.segment_sum(msg, edge_dst, num_segments=N)
            gi = m_agg @ w_ih.T + b_ih
            gh = h @ w_hh.T + b_hh
            i_r, i_z, i_n = (gi[:, :H], gi[:, H:2 * H], gi[:, 2 * H:])
            h_r, h_z, h_n = (gh[:, :H], gh[:, H:2 * H], gh[:, 2 * H:])
            r = jax.nn.sigmoid(i_r + h_r)
            z = jax.nn.sigmoid(i_z + h_z)
            n = jnp.tanh(i_n + r * h_n)
            return (1.0 - z) * n + z * h
        return _ggnn_forward(h, edge_matrix, w_ih, w_hh, b_ih, b_hh, edge_src, edge_dst, edge_type)

    def _L2_gnn_ref(h, src, dst, Wq, Wk, Wv, Wo, gamma, beta):
        import jax, jax.numpy as jnp
        import numpy as np
        N, E, H, D = (50000, 12500, 4, 64)
        IN = D
        EPS = 1e-05
        n = h.shape[0]
        Q = (h @ Wq).reshape(n, H, D)
        K = (h @ Wk).reshape(n, H, D)
        V = (h @ Wv).reshape(n, H, D)
        score = jnp.einsum('ehd,ehd->eh', Q[src], K[dst]) / np.sqrt(D)
        attn = jax.nn.softmax(score, axis=1)
        m = V[src] * attn[:, :, None]
        h_new = jax.ops.segment_sum(m, dst, num_segments=n)
        h_proj = h_new.reshape(n, H * D) @ Wo
        x = h_proj + h
        mu = jnp.mean(x, axis=-1, keepdims=True)
        var = jnp.mean((x - mu) ** 2, axis=-1, keepdims=True)
        return (x - mu) * jax.lax.rsqrt(var + EPS) * gamma + beta

    def _L3_gnn_ref(feat, W1, W2, src, dst):
        import jax, jax.numpy as jnp
        import numpy as np
        N_NODES = 100000
        N_EDGES = 25000
        D_IN = 64
        D_OUT = 64
        LEAKY_SLOPE = 0.01
        N = feat.shape[0]
        ones = jnp.ones(src.shape[0], dtype=feat.dtype)
        deg = jnp.maximum(jax.ops.segment_sum(ones, src, num_segments=N), 1.0)
        self_term = feat @ W1
        inter = self_term[src] + feat[src] * feat[dst] @ W2
        norm = jnp.sqrt(deg[src] * deg[dst])[:, None]
        msg = inter / norm
        agg = jax.ops.segment_sum(msg, dst, num_segments=N)
        embed = self_term + agg
        return jax.nn.leaky_relu(embed, negative_slope=LEAKY_SLOPE)
    edge_index = jnp.stack([src, dst])
    h = jnp.maximum(_layernorm(x, axis=-1), 0.0)
    x = x + _L0_gnn_ref(h, edge_index, L0_gnn_W, L0_gnn_b)
    h = jnp.maximum(_layernorm(x, axis=-1), 0.0)
    x = x + _L1_gnn_ref(h, L1_gnn_edge_matrix, L1_gnn_w_ih, L1_gnn_w_hh, L1_gnn_b_ih, L1_gnn_b_hh, src, dst, edge_type_8)
    h = jnp.maximum(_layernorm(x, axis=-1), 0.0)
    x = x + _L2_gnn_ref(h, src, dst, L2_gnn_Wq, L2_gnn_Wk, L2_gnn_Wv, L2_gnn_Wo, L2_gnn_gamma, L2_gnn_beta)
    h = jnp.maximum(_layernorm(x, axis=-1), 0.0)
    x = x + _L3_gnn_ref(h, L3_gnn_W1, L3_gnn_W2, src, dst)
    return x

_drawn_inputs = setup_inputs


def setup_inputs(seed=0):
    import zlib

    import numpy as np

    out = dict(_drawn_inputs(seed))
    spreads = {'L2_gnn_gamma': (1.0, 0.2), 'L2_gnn_beta': (0.0, 0.1)}
    factors = {'L2_gnn_Wq': 8.0, 'L2_gnn_Wk': 8.0}
    for name, (base, spread) in spreads.items():
        noise = np.random.default_rng([zlib.crc32(name.encode()), seed]).standard_normal(out[name].shape)
        drawn = base * np.exp(spread * noise) if base else spread * noise
        out[name] = jnp.asarray(drawn.astype(out[name].dtype))
    for name, factor in factors.items():
        out[name] = (out[name] * factor).astype(out[name].dtype)
    return out
```

```python
from contextlib import ExitStack

import concourse.bass as bass
from concourse import mybir

F32 = mybir.dt.float32
BF16 = mybir.dt.bfloat16
FP16 = mybir.dt.float16
I32 = mybir.dt.int32
U32 = mybir.dt.uint32
ALU = mybir.AluOpType
ACT = mybir.ActivationFunctionType
AX = mybir.AxisListType

P = 128
F = 64
HEADS = 4
TYPES = 8
DEPTH = 3
TILES = 4
SLOTS = 16
HALF = SLOTS // 2
LEAKY = 0.01
EPS = 1e-5


class Signal:

    def __init__(self, handle):
        self.sem, self.base = handle, 0


def given(value):
    return not isinstance(value, int) or value > 0


def at(i, q, delta=0):
    return (q + delta) % DEPTH, DEPTH * i + (q + delta), i + (q + delta) // DEPTH + 1


def rounds(engine, body, steps):
    last = (steps - 1) // DEPTH
    for q in range(DEPTH):
        body(0, q)
    with engine.Fori(1, last, 1) as i:
        for q in range(DEPTH):
            body(i, q)
    for q in range(steps - DEPTH * last):
        body(last, q)


def graph_layers(nc, x, src, dst, edge_type, w0t, b0, at_w, w_iht, w_hht, b_ih, b_hh,
                 wqt, wkt, wvt, wo, gamma, beta, w1, w2, out):
    N, E = x.shape[0], src.shape[0]
    BATCH = P * SLOTS
    BATCHES = -(-N // BATCH)
    NP = BATCHES * BATCH
    COLS = BATCHES * SLOTS
    LAST_P = (N - (BATCHES - 1) * BATCH) // SLOTS
    assert (N - (BATCHES - 1) * BATCH) % SLOTS == 0 and BATCHES % DEPTH == 1
    GROUP = TILES * P
    NR = NP + GROUP
    EFULL = E // P
    EREST = E - EFULL * P
    GROUPS = -(-(EFULL + 1) // TILES)
    GROUPS = -(-GROUPS // DEPTH) * DEPTH
    ECOLS = GROUPS * TILES

    def dram(name, shape):
        return nc.dram_tensor(name, shape, F32, kind="Internal").ap()

    t0 = dram("t0", (NR, F))
    acc0 = dram("acc0", (NR, F))
    x1 = dram("x1", (NP, F))
    mh1 = dram("mh1", (NR, 2 * F))
    x2 = dram("x2", (NP, F))
    h2 = dram("h2", (NR, F))
    acc2 = dram("acc2", (NR, F))
    x3 = dram("x3", (NP, F))
    u3 = dram("u3", (NR, F))
    acc3 = dram("acc3", (NR, F))
    mh1_rows = mh1.rearrange("n (k f) -> (n k) f", k=2)

    root = ExitStack()
    with root:
        def sb(name, shape, dt=F32, ctx=root):
            return ctx.enter_context(nc.sbuf_tensor(name, shape, dt))

        def ps(name, shape, ctx, dt=F32):
            return ctx.enter_context(nc.psum_tensor(name, shape, dt))

        def signal(name):
            return Signal(root.enter_context(nc.semaphore(name)))

        def signals(name, n=DEPTH):
            return [signal(f"{name}{k}") for k in range(n)]

        ident = sb("ident", [P, P])
        src_row = sb("src_row", [P, ECOLS], I32)
        dst_row = sb("dst_row", [P, ECOLS], I32)
        src_key = sb("src_key", [P, ECOLS])
        dst_key = sb("dst_key", [P, ECOLS])
        type_f = sb("type_f", [P, ECOLS])
        src_into = sb("src_into", [P, ECOLS], I32)
        dst_into = sb("dst_into", [P, ECOLS], I32)
        spare = sb("spare", [P, TILES])
        earlier = sb("earlier", [P, P], BF16)
        ones = sb("ones", [P, 1], BF16)
        ident_b = sb("ident_b", [P, P], BF16)
        dinv = sb("dinv", [P, COLS])
        inv_s = sb("inv_s", [P, COLS])
        sqrt_s = sb("sqrt_s", [P, COLS])
        w0_pair = sb("w0_pair", [P, P])
        ones3 = sb("ones3", [3, P], BF16)
        b0_parts = sb("b0_parts", [3, 8 * F], BF16)
        gate_w = sb("gate_w", [P, 4 * F])
        gate_b_parts = sb("gate_b_parts", [3, 8 * F], BF16)
        type_w = sb("type_w", [P, TYPES // 2, F])
        type_of = sb("type_of", [P, TYPES // 2])
        att_w = sb("att_w", [F, 2 * HEADS * F])
        gb_rows = sb("gb_rows", [P, 2, F])
        w12 = sb("w12", [P, F])
        eps_t = sb("eps_t", [P, 1])

        rows_staged = signal("rows_staged")
        turn = signal("turn")
        gathered = signals("gathered")
        keys_spread = signal("keys_spread")
        matched = signal("matched")
        diagonal = signal("diagonal")
        counted = signal("counted")
        spared = signal("spared")
        chosen = signal("chosen")
        into_known = signal("into_known")
        into_staged = signal("into_staged")
        summed = signal("summed")
        sums_copied = signal("sums_copied")
        scattered = signals("scattered")
        turned = signal("turned")
        turned_copied = signal("turned_copied")
        types_spread = signal("types_spread")
        by_type = signal("by_type")
        messages_turned = signal("messages_turned")
        messages_copied = signal("messages_copied")
        messages = signal("messages")
        first_part = signal("first_part")
        rest_left = signal("rest_left")
        second_part = signal("second_part")
        parts_made = signal("parts_made")
        projected = signal("projected")
        att = signals("att_step", 8)

        loaded = signals("loaded")
        stored = signals("stored")
        mixed = signal("mixed")
        x_new = signal("x_new")
        ln = [[signal(f"ln{k}_{s}") for s in ("sum", "centred", "squared", "var", "std", "rstd")]
              for k in range(2)]
        h_new = signal("h_new")
        node_turned = signal("node_turned")
        node_copied = signal("node_copied")
        node_out = signal("node_out")
        t_done = signal("t_done")
        step = signals("node_step", 6)

        def advance(counts):
            for s, n in counts:
                s.base += n

        with ExitStack() as ctx:
            raw = sb("raw", [P, 3, ECOLS], I32, ctx)
            n_mask = sb("n_mask", [P, ECOLS], I32, ctx)
            hi_i = sb("hi_i", [P, ECOLS], I32, ctx)
            lo_i = sb("lo_i", [P, 2, ECOLS], I32, ctx)
            hi_f = sb("hi_f", [P, ECOLS], F32, ctx)
            lo_f = sb("lo_f", [P, ECOLS], F32, ctx)
            iota_i = sb("iota_i", [P, COLS], I32, ctx)
            iota = sb("iota", [P, COLS], FP16, ctx)
            type_i = sb("type_i", [P, TYPES // 2], I32, ctx)
            type_h = sb("type_h", [P, TYPES // 2], I32, ctx)
            spare_i = sb("spare_i", [P, TILES], I32, ctx)
            hot_p = sb("hot_p", [P, TILES, P], BF16, ctx)
            hot_c = sb("hot_c", [P, TILES, COLS], BF16, ctx)
            zero = sb("zero", [P, BATCH * F // P], F32, ctx)
            bias = sb("bias", [1, 2, 3 * F], F32, ctx)
            b_gate = sb("b_gate", [1, 4 * F], F32, ctx)
            b_zero = sb("b_zero", [1, F], F32, ctx)
            part = sb("part", [1, 2, 3, 8 * F], BF16, ctx)
            rest = sb("rest", [1, 2, 2, 8 * F], F32, ctx)
            b_rep = sb("b_rep", [1, 2, 8 * F], F32, ctx)
            wq_s = sb("wq_s", [F, HEADS, F], F32, ctx)
            wk_s = sb("wk_s", [F, HEADS, F], F32, ctx)
            wv_s = sb("wv_s", [F, HEADS, F], F32, ctx)
            wo_s = sb("wo_s", [F, HEADS, F], F32, ctx)
            cnt1 = sb("cnt1", [P, COLS], F32, ctx)
            cnt2 = sb("cnt2", [P, COLS], F32, ctx)
            p_half = sb("p_half", [P, COLS], F32, ctx)
            m_half = sb("m_half", [P, COLS], F32, ctx)
            count_ps = [ps(f"count_ps{k}", [P, COLS // 2], ctx) for k in range(2)]
            att_ps = ps("att_ps", [F, 512], ctx)

            own = ExitStack()

            def local(name):
                return Signal(ctx.enter_context(nc.semaphore(name)))

            raw_set = local("raw_set")
            raw_in = local("raw_in")
            zero_set = local("zero_set")
            zeroed = local("zeroed")
            w_clear = local("w_clear")
            w_in = local("w_in")
            parts_done = local("parts_done")
            parts_moved = local("parts_moved")
            v_step = local("v_step")
            g_step = local("g_step")
            keys_done = local("keys_done")
            hot = local("hot")
            tile_counted = local("tile_counted")
            att_out = local("att_out")
            att_copied = local("att_copied")

            block = ctx.enter_context(nc.Block())

            @block.sync
            def _(sp):
                sp.wait_ge(raw_set.sem, raw_set.base + 2)
                for k, a in enumerate((src, dst, edge_type)):
                    sp.dma_start(raw[:, k, 0:EFULL], a[0:P * EFULL].rearrange("(p t) -> p t", t=EFULL)).then_inc(raw_in.sem, 16)
                    sp.dma_start(raw[0:EREST, k, EFULL:EFULL + 1], a[P * EFULL:E].rearrange("(p t) -> p t", t=1)).then_inc(raw_in.sem, 16)
                sp.wait_ge(w_clear.sem, w_clear.base + 2)
                sp.dma_start(w0_pair[0:F, 0:F], w0t).then_inc(w_in.sem, 16)
                sp.dma_start(w0_pair[F:P, F:P], w0t).then_inc(w_in.sem, 16)
                sp.dma_start(gate_w[0:F, 0:3 * F], w_iht).then_inc(w_in.sem, 16)
                sp.dma_start(gate_w[F:P, 0:2 * F], w_hht[:, 0:2 * F]).then_inc(w_in.sem, 16)
                sp.dma_start(gate_w[F:P, 3 * F:4 * F], w_hht[:, 2 * F:3 * F]).then_inc(w_in.sem, 16)
                sp.dma_start(type_w[:, :, :], at_w.rearrange("(c p) m -> p c m", p=P)).then_inc(w_in.sem, 16)
                for s, w in ((wq_s, wqt), (wk_s, wkt), (wv_s, wvt), (wo_s, wo)):
                    sp.dma_start(s[:, :, :], w.rearrange("(h d) j -> d h j", h=HEADS)).then_inc(w_in.sem, 16)
                sp.dma_start(w12[0:F, :], w1).then_inc(w_in.sem, 16)
                sp.dma_start(w12[F:P, :], w2).then_inc(w_in.sem, 16)
                for k, a in enumerate((gamma, beta)):
                    sp.dma_start(gb_rows[:, k, :], a.rearrange("(a f) -> a f", a=1).to_broadcast([P, F])).then_inc(w_in.sem, 16)
                for k, a in enumerate((b_ih, b_hh)):
                    sp.dma_start(bias[0:1, k, :], a.rearrange("(a f) -> a f", a=1)).then_inc(w_in.sem, 16)
                sp.dma_start(b_zero[0:1, :], b0.rearrange("(a f) -> a f", a=1)).then_inc(w_in.sem, 16)
                sp.wait_ge(parts_done.sem, parts_done.base + 3)
                for k, b in enumerate((b0_parts, gate_b_parts)):
                    for j in range(3):
                        sp.dma_start(b[j:j + 1, :], part[0:1, k, j, :]).then_inc(parts_moved.sem, 16)
                sp.wait_ge(zero_set.sem, zero_set.base + 1)
                for b in range(BATCHES):
                    sp.dma_start(acc3[b * BATCH:(b + 1) * BATCH, :].rearrange("(p g) f -> p (g f)", p=P), zero[:, :]).then_inc(zeroed.sem, 16)
                for t in (t0, acc0, mh1, h2, acc2, u3, acc3):
                    w = (NR - NP) * t.shape[1] // P
                    sp.dma_start(t[NP:NR, :].rearrange("(p g) f -> p (g f)", p=P), zero[:, 0:w]).then_inc(zeroed.sem, 16)
                sp.wait_ge(parts_moved.sem, parts_moved.base + 6 * 16)
                sp.wait_ge(zeroed.sem, zeroed.base + (BATCHES + 7) * 16)

            @block.gpsimd
            def _(pool):
                pool.iota(raw[:, 0, :], [[0, ECOLS // TILES], [P, TILES]], base=NP, channel_multiplier=1).then_inc(raw_set.sem, 1)
                pool.iota(raw[:, 1, :], [[0, ECOLS // TILES], [P, TILES]], base=NP, channel_multiplier=1).then_inc(raw_set.sem, 1)
                pool.iota(spare_i[:, :], [[P, TILES]], base=NP, channel_multiplier=1).then_inc(g_step.sem, 1)
                pool.iota(iota_i[:, :], [[1, COLS]], base=0, channel_multiplier=0).then_inc(g_step.sem, 1)
                pool.iota(type_i[:, :], [[P, TYPES // 2]], base=0, channel_multiplier=1).then_inc(g_step.sem, 1)
                pool.memset(ident[:, :], 0.0).then_inc(g_step.sem, 1)
                pool.memset(earlier[:, :], 1.0).then_inc(g_step.sem, 1)
                pool.memset(ident_b[:, :], 0.0).then_inc(g_step.sem, 1)
                pool.wait_ge(g_step.sem, g_step.base + 6)
                pool.affine_select(out=ident_b[:, :], in_=ident_b[:, :], compare_op=ALU.not_equal, fill=1.0,
                                   base=0, pattern=[[-1, P]], channel_multiplier=1).then_inc(g_step.sem, 1)
                pool.affine_select(out=ident[:, :], in_=ident[:, :], compare_op=ALU.not_equal, fill=1.0,
                                   base=0, pattern=[[-1, P]], channel_multiplier=1).then_inc(g_step.sem, 1)
                pool.affine_select(out=earlier[:, :], in_=earlier[:, :], compare_op=ALU.is_gt, fill=0.0,
                                   base=0, pattern=[[1, P]], channel_multiplier=-1).then_inc(g_step.sem, 1)
                pool.memset(eps_t[:, :], EPS)
                pool.memset(ones[:, :], 1.0)
                pool.memset(p_half[:, :], 0.5)
                pool.memset(m_half[:, :], -0.5).then_inc(g_step.sem, 1)
                pool.wait_ge(g_step.sem, g_step.base + 10)
                pool.wait_ge(v_step.sem, v_step.base + 12)
                pool.tensor_tensor(dinv[:, :], cnt1[:, :], m_half[:, :], ALU.pow)
                pool.tensor_tensor(inv_s[:, :], cnt2[:, :], m_half[:, :], ALU.pow)
                pool.tensor_tensor(sqrt_s[:, :], cnt2[:, :], p_half[:, :], ALU.pow)

            @block.scalar
            def _(act):
                act.wait_ge(att_out.sem, att_out.base + 1)
                act.activation(att_w[:, 0:HEADS * F], att_ps[:, 0:HEADS * F], ACT.Copy, scale=float(F) ** -0.5).then_inc(att_copied.sem, 1)
                act.activation(att_w[:, HEADS * F:2 * HEADS * F], att_ps[:, HEADS * F:2 * HEADS * F], ACT.Copy).then_inc(att_copied.sem, 1)

            @block.tensor
            def _(pe):
                pe.wait_ge(w_in.sem, w_in.base + 17 * 16)
                for h in range(HEADS):
                    pe.matmul(att_ps[:, h * F:(h + 1) * F], wq_s[:, h, :], wk_s[:, h, :], start=True, stop=True)
                for h in range(HEADS):
                    last = pe.matmul(att_ps[:, (HEADS + h) * F:(HEADS + h + 1) * F], wv_s[:, h, :], wo_s[:, h, :], start=True, stop=True)
                last.then_inc(att_out.sem, 1)

                def count(i, k, first, final):
                    pe.wait_ge(hot.sem, hot.base + i * TILES + k + 1)
                    for j in range(2):
                        w = COLS // 2
                        last = pe.matmul(count_ps[j][:, :], hot_p[:, k, :], hot_c[:, k, j * w:(j + 1) * w], start=first, stop=final)
                    last.then_inc(tile_counted.sem, 1)

                for k in range(TILES):
                    count(0, k, k == 0, False)
                with pe.Fori(1, GROUPS - 1, 1) as i:
                    for k in range(TILES):
                        count(i, k, False, False)
                for k in range(TILES):
                    count(GROUPS - 1, k, False, k == TILES - 1)

            @block.vector
            def _(dve):
                steps = [0]

                def then(ins):
                    ins.then_inc(v_step.sem, 1)
                    steps[0] += 1

                def after():
                    dve.wait_ge(v_step.sem, v_step.base + steps[0])

                dve.memset(zero[:, :], 0.0).then_inc(zero_set.sem, 1)
                dve.memset(w0_pair[:, :], 0.0).then_inc(w_clear.sem, 1)
                dve.memset(gate_w[:, :], 0.0).then_inc(w_clear.sem, 1)
                dve.memset(ones3[:, :], 1.0)
                dve.wait_ge(raw_in.sem, raw_in.base + 6 * 16)
                dve.wait_ge(g_step.sem, g_step.base + 5)
                slot_bits, part_bits = SLOTS.bit_length() - 1, P.bit_length() - 1
                then(dve.tensor_scalar(hi_i[:, :], raw[:, 0, :], slot_bits, P - 1, ALU.logical_shift_right, ALU.bitwise_and))
                then(dve.tensor_scalar(lo_i[:, 0, :], raw[:, 0, :], slot_bits + part_bits, slot_bits, ALU.logical_shift_right, ALU.logical_shift_left))
                then(dve.tensor_scalar(lo_i[:, 1, :], raw[:, 0, :], SLOTS - 1, None, ALU.bitwise_and))
                after()
                then(dve.tensor_copy(hi_f[:, :], hi_i[:, :]))
                then(dve.tensor_tensor(lo_f[:, :], lo_i[:, 0, :], lo_i[:, 1, :], ALU.add))
                then(dve.tensor_copy(iota[:, :], iota_i[:, :]))
                after()

                def one_hot(i, k):
                    if given((i - 1) * TILES + k + 1):
                        dve.wait_ge(tile_counted.sem, tile_counted.base + (i - 1) * TILES + k + 1)
                    col = i * TILES + k
                    dve.tensor_scalar(hot_p[:, k, :], iota[:, 0:P], hi_f[:, bass.ds(col, 1)], None, ALU.is_equal)
                    dve.tensor_scalar(hot_c[:, k, :], iota[:, :], lo_f[:, bass.ds(col, 1)], None, ALU.is_equal).then_inc(hot.sem, 1)

                for k in range(TILES):
                    one_hot(0, k)
                with dve.Fori(1, GROUPS, 1) as i:
                    for k in range(TILES):
                        one_hot(i, k)

                dve.tensor_copy(src_key[:, :], raw[:, 0, :])
                dve.tensor_copy(dst_key[:, :], raw[:, 1, :])
                dve.memset(src_row[:, :], 0)
                dve.memset(dst_row[:, :], 0)
                dve.memset(type_f[:, :], 0.0)
                then(dve.tensor_copy(spare[:, :], spare_i[:, :]))
                after()
                for a, k in ((src_row, 0), (dst_row, 1), (type_f, 2)):
                    dve.tensor_copy(a[:, 0:EFULL], raw[:, k, 0:EFULL])
                    dve.tensor_copy(a[0:EREST, EFULL:EFULL + 1], raw[0:EREST, k, EFULL:EFULL + 1])
                dve.memset(src_into[:, :], 0)
                dve.memset(dst_into[:, :], 0)
                then(dve.tensor_scalar(type_h[:, :], type_i[:, :], 6, None, ALU.logical_shift_right))
                dve.wait_ge(w_in.sem, w_in.base + 17 * 16)
                dve.tensor_tensor(b_gate[0:1, 0:2 * F], bias[0:1, 0, 0:2 * F], bias[0:1, 1, 0:2 * F], ALU.add)
                dve.tensor_copy(b_gate[0:1, 2 * F:3 * F], bias[0:1, 0, 2 * F:3 * F])
                then(dve.tensor_copy(b_gate[0:1, 3 * F:4 * F], bias[0:1, 1, 2 * F:3 * F]))
                after()
                dve.tensor_copy(type_of[:, :], type_h[:, :])
                dve.tensor_copy(b_rep[0:1, 0, :].rearrange("p (r f) -> p r f", r=8), b_zero[0:1, :].unsqueeze(1).to_broadcast([1, 8, F]))
                then(dve.tensor_copy(b_rep[0:1, 1, :].rearrange("p (r f) -> p r f", r=2), b_gate[0:1, :].unsqueeze(1).to_broadcast([1, 2, 4 * F])))
                after()
                dve.tensor_copy(part[0:1, :, 0, :], b_rep[0:1, :, :]).then_inc(parts_done.sem, 1)
                dve.wait_ge(parts_done.sem, parts_done.base + 1)
                then(dve.tensor_tensor(rest[0:1, 0, :, :], b_rep[0:1, :, :], part[0:1, :, 0, :], ALU.subtract))
                after()
                dve.tensor_copy(part[0:1, :, 1, :], rest[0:1, 0, :, :]).then_inc(parts_done.sem, 1)
                dve.wait_ge(parts_done.sem, parts_done.base + 2)
                dve.tensor_tensor(rest[0:1, 1, :, :], rest[0:1, 0, :, :], part[0:1, :, 1, :], ALU.subtract).then_inc(keys_done.sem, 1)
                dve.wait_ge(keys_done.sem, keys_done.base + 1)
                dve.tensor_copy(part[0:1, :, 2, :], rest[0:1, 1, :, :]).then_inc(parts_done.sem, 1)
                dve.wait_ge(tile_counted.sem, tile_counted.base + GROUPS * TILES)
                for j in range(2):
                    w = COLS // 2
                    dve.tensor_scalar(cnt1[:, j * w:(j + 1) * w], count_ps[j][:, :], 1.0, None, ALU.add)
                    last = dve.tensor_scalar(cnt2[:, j * w:(j + 1) * w], count_ps[j][:, :], 1.0, None, ALU.max)
                then(last)
                assert steps[0] == 12

        def batch(t, b):
            return t[bass.ds(b * BATCH, BATCH), :].rearrange("(p g) f -> p (g f)", p=P)

        def last_batch(t):
            return t[(BATCHES - 1) * BATCH:N, :].rearrange("(p g) f -> p (g f)", g=SLOTS)

        def halves(a, width=F):
            return a.rearrange("p (g f) -> p g f", f=width)

        def node_streams(sp, loads, stores, freed, done):
            def load(i, q):
                slot, b, _ = at(i, q)
                if given(2 * (b - DEPTH) + 2):
                    sp.wait_ge(freed.sem, freed.base + 2 * (b - DEPTH) + 2)
                for table, tile in loads:
                    if isinstance(b, int) and b == BATCHES - 1 and table.shape[0] == N:
                        sp.dma_start(tile[0:LAST_P, slot, :], last_batch(table)).then_inc(loaded[slot].sem, 16)
                    else:
                        sp.dma_start(tile[:, slot, :], batch(table, b)).then_inc(loaded[slot].sem, 16)

            def store(i, q):
                slot, b, _ = at(i, q)
                sp.wait_ge(done.sem, done.base + 2 * b + 2)
                for table, tile in stores:
                    if isinstance(b, int) and b == BATCHES - 1 and table.shape[0] == N:
                        sp.dma_start(last_batch(table), tile[0:LAST_P, slot, :]).then_inc(stored[slot].sem, 16)
                    else:
                        sp.dma_start(batch(table, b), tile[:, slot, :]).then_inc(stored[slot].sem, 16)

            def body(i, q):
                load(i + (q + 1) // DEPTH, (q + 1) % DEPTH)
                if q or not isinstance(i, int) or i:
                    store(i + (q - 1) // DEPTH, (q - 1) % DEPTH)

            R = BATCHES // DEPTH
            load(0, 0)
            for q in range(DEPTH):
                body(0, q)
            with sp.Fori(1, R - 1, 1) as i:
                for q in range(DEPTH):
                    body(i, q)
            for q in range(DEPTH):
                body(R - 1, q)
            store(R - 1, DEPTH - 1)
            store(R, 0)
            for slot in range(DEPTH):
                sp.wait_ge(stored[slot].sem, stored[slot].base + 16 * len(stores) * (R + (slot == 0)))

        def stored_before(engine, i, q, n_stores):
            slot, _, uses = at(i, q, -DEPTH)
            if given(uses * 16 * n_stores):
                engine.wait_ge(stored[slot].sem, stored[slot].base + uses * 16 * n_stores)

        def node_signals(n_loads, n_stores):
            R = BATCHES // DEPTH
            return ([(loaded[s], 16 * n_loads * (R + (s == 0))) for s in range(DEPTH)]
                    + [(stored[s], 16 * n_stores * (R + (s == 0))) for s in range(DEPTH)])

        LN_SUM, LN_CENTRED, LN_SQUARED, LN_VAR, LN_STD, LN_RSTD = range(6)

        class Norm:

            def __init__(self, k, ctx, pre):
                self.s = ln[k]
                self.sum = sb(f"{pre}_sum", [P, 2, HALF], F32, ctx)
                self.xc = sb(f"{pre}_xc", [P, 2, HALF, F], F32, ctx)
                self.sq = sb(f"{pre}_sq", [P, 2, HALF, F], F32, ctx)
                self.var = sb(f"{pre}_var", [P, 2, HALF], F32, ctx)
                self.std = sb(f"{pre}_std", [P, 2, HALF], F32, ctx)
                self.rstd = sb(f"{pre}_rstd", [P, 2, HALF], F32, ctx)

            def dve_sum(self, dve, n, s, xs):
                dve.tensor_reduce(self.sum[:, s, :], xs, AX.X, ALU.add).then_inc(self.s[LN_SUM].sem, 1)

            def dve_centre(self, dve, n, s, xs):
                dve.wait_ge(self.s[LN_SUM].sem, self.s[LN_SUM].base + n + 1)
                dve.scalar_tensor_tensor(out=self.xc[:, s, :, :], in0=self.sum[:, s, :].unsqueeze(2).to_broadcast([P, HALF, F]),
                                         scalar=-1.0 / F, in1=xs, op0=ALU.mult, op1=ALU.add).then_inc(self.s[LN_CENTRED].sem, 1)

            def act_square(self, act, n, s):
                act.wait_ge(self.s[LN_CENTRED].sem, self.s[LN_CENTRED].base + n + 1)
                if given(n - 1):
                    act.wait_ge(self.s[LN_VAR].sem, self.s[LN_VAR].base + n - 1)
                act.activation(self.sq[:, s, :, :], self.xc[:, s, :, :], ACT.Square, scale=float(F) ** -0.5).then_inc(self.s[LN_SQUARED].sem, 1)

            def dve_var(self, dve, n, s):
                dve.wait_ge(self.s[LN_SQUARED].sem, self.s[LN_SQUARED].base + n + 1)
                dve.tensor_reduce(self.var[:, s, :], self.sq[:, s, :, :], AX.X, ALU.add).then_inc(self.s[LN_VAR].sem, 1)

            def act_std(self, act, n, s):
                act.wait_ge(self.s[LN_VAR].sem, self.s[LN_VAR].base + n + 1)
                if given(n - 1):
                    act.wait_ge(self.s[LN_RSTD].sem, self.s[LN_RSTD].base + n - 1)
                act.activation(self.std[:, s, :], self.var[:, s, :], ACT.Sqrt, bias=eps_t[:, 0:1]).then_inc(self.s[LN_STD].sem, 1)

            def dve_rstd(self, dve, n, s):
                dve.wait_ge(self.s[LN_STD].sem, self.s[LN_STD].base + n + 1)
                dve.reciprocal(self.rstd[:, s, :], self.std[:, s, :]).then_inc(self.s[LN_RSTD].sem, 1)

            def dve_relu(self, dve, n, s, outs, scale=None, ready=None):
                ready = ready or self.s[LN_RSTD]
                dve.wait_ge(ready.sem, ready.base + n + 1)
                scale = self.rstd[:, s, :] if scale is None else scale
                return dve.scalar_tensor_tensor(out=outs, in0=self.xc[:, s, :, :], scalar=0.0,
                                                in1=scale.unsqueeze(2).to_broadcast([P, HALF, F]), op0=ALU.max, op1=ALU.mult)

            def totals(self):
                return [(s, 2 * BATCHES) for s in self.s]

        def gate(engine):
            engine.sem_inc(turn.sem, 1)

        def cols(i, q, s):
            _, b, _ = at(i, q)
            return bass.ds(b * SLOTS + s * HALF, HALF)

        def spread(a):
            return a.unsqueeze(2).to_broadcast([P, HALF, F])

        with ExitStack() as ctx:
            x_in = sb("p0_x", [P, DEPTH, SLOTS * F], F32, ctx)
            h_t = sb("p0_h", [P, DEPTH, SLOTS * F], F32, ctx)
            t_out = sb("p0_t", [P, DEPTH, SLOTS * F], F32, ctx)
            hT = sb("p0_hT", [P, 2, 512], F32, ctx)
            turn_ps = [ps(f"p0_turn{k}", [P, 512], ctx) for k in range(2)]
            lin_ps = [ps(f"p0_lin{k}", [P, 512], ctx) for k in range(2)]
            norm = Norm(0, ctx, "p0")
            block = ctx.enter_context(nc.Block())

            def half(tile, slot, s):
                return halves(tile[:, slot, s * HALF * F:(s + 1) * HALF * F])

            @block.sync
            def _(sp):
                node_streams(sp, [(x, x_in)], [(t0, t_out), (acc0, t_out)], ln[0][LN_CENTRED], t_done)

            @block.vector
            def _(dve):
                def finish(i, q):
                    slot, b, _ = at(i, q)
                    stored_before(dve, i, q, 2)
                    for s in range(2):
                        dve.wait_ge(node_out.sem, node_out.base + 2 * b + s + 1)
                        dve.tensor_tensor(half(t_out, slot, s), halves(lin_ps[s][:, :]), spread(dinv[:, cols(i, q, s)]), ALU.mult).then_inc(t_done.sem, 1)

                def body(i, q):
                    slot, b, uses = at(i, q)
                    dve.wait_ge(loaded[slot].sem, loaded[slot].base + 16 * uses)
                    for s in range(2):
                        norm.dve_sum(dve, 2 * b + s, s, half(x_in, slot, s))
                    for s in range(2):
                        norm.dve_centre(dve, 2 * b + s, s, half(x_in, slot, s))
                    for s in range(2):
                        norm.dve_var(dve, 2 * b + s, s)
                    if q or not isinstance(i, int) or i:
                        finish(i + (q - 1) // DEPTH, (q - 1) % DEPTH)
                    for s in range(2):
                        norm.dve_rstd(dve, 2 * b + s, s)
                    if given(2 * (b - DEPTH) + 2):
                        dve.wait_ge(node_turned.sem, node_turned.base + 2 * (b - DEPTH) + 2)
                    for s in range(2):
                        norm.dve_relu(dve, 2 * b + s, s, half(h_t, slot, s)).then_inc(h_new.sem, 1)

                rounds(dve, body, BATCHES)
                finish(BATCHES // DEPTH, 0)

            @block.scalar
            def _(act):
                def body(i, q):
                    _, b, _ = at(i, q)
                    for s in range(2):
                        norm.act_square(act, 2 * b + s, s)
                    for s in range(2):
                        norm.act_std(act, 2 * b + s, s)
                    for s in range(2):
                        act.wait_ge(node_turned.sem, node_turned.base + 2 * b + s + 1)
                        if given(2 * b + s - 1):
                            act.wait_ge(node_out.sem, node_out.base + 2 * b + s - 1)
                        act.activation(hT[:, s, :], turn_ps[s][:, :], ACT.Copy).then_inc(node_copied.sem, 1)

                rounds(act, body, BATCHES)

            @block.tensor
            def _(pe):
                def body(i, q):
                    slot, b, _ = at(i, q)
                    for s in range(2):
                        pe.wait_ge(h_new.sem, h_new.base + 2 * b + s + 1)
                        if given(2 * b + s - 1):
                            pe.wait_ge(node_copied.sem, node_copied.base + 2 * b + s - 1)
                        for k in range(4):
                            at_k = (s * HALF + 2 * k) * F
                            last = pe.transpose(turn_ps[s][:, k * P:(k + 1) * P], h_t[:, slot, at_k:at_k + P], ident[:, :])
                        last.then_inc(node_turned.sem, 1)
                    for s in range(2):
                        pe.wait_ge(node_copied.sem, node_copied.base + 2 * b + s + 1)
                        if given(2 * b + s - 1):
                            pe.wait_ge(t_done.sem, t_done.base + 2 * b + s - 1)
                        pe.matmul(lin_ps[s][:, :], ones3[:, :], b0_parts[:, :], start=True, stop=False, skip_group_check=True)
                        for k in range(4):
                            last = pe.matmul(lin_ps[s][:, k * P:(k + 1) * P], hT[:, s, k * P:(k + 1) * P], w0_pair[:, :],
                                             start=False, stop=k == 3, skip_group_check=True)
                        last.then_inc(node_out.sem, 1)

                rounds(pe, body, BATCHES)

            advance(node_signals(1, 2) + norm.totals()
                    + [(s, 2 * BATCHES) for s in (t_done, h_new, node_turned, node_copied, node_out)])

        def edge_phase(pre, gathers, key, into, into_scale, table, find_into, kind):
            NG = len(gathers)
            AHEAD = 2 if kind == "types" else 1
            LAG = AHEAD + 1
            with ExitStack() as ctx:
                stage = sb(f"{pre}_stage", [P, DEPTH, NG, TILES], I32, ctx)
                keys = sb(f"{pre}_keys", [P, DEPTH, TILES], F32, ctx)
                types = sb(f"{pre}_types", [P, DEPTH, TILES], BF16, ctx) if kind == "types" else None
                into_st = sb(f"{pre}_into", [P, DEPTH, TILES], I32, ctx)
                got = [sb(f"{pre}_got{k}", [P, DEPTH, TILES, F], F32, ctx) for k in range(NG)]
                match = sb(f"{pre}_match", [P, DEPTH, TILES, GROUP], BF16, ctx)
                sums = sb(f"{pre}_sums", [P, DEPTH, TILES * F], F32, ctx)
                diag = sb(f"{pre}_diag", [P, TILES, P], BF16, ctx)
                count_ps = ps(f"{pre}_count", [P, TILES], ctx) if find_into else None
                gap = sb(f"{pre}_gap", [P, TILES], F32, ctx)
                move = sb(f"{pre}_move", [P, TILES], F32, ctx)
                rows_ps = ps(f"{pre}_rows", [P, GROUP], ctx)
                sum_ps = ps(f"{pre}_sum", [P, TILES * F], ctx)
                parts = sb(f"{pre}_parts", [P, DEPTH, 3, TILES * F], BF16, ctx)
                rest = sb(f"{pre}_rest", [P, TILES * F], F32, ctx)
                if kind == "types":
                    type_ps = ps(f"{pre}_type", [P, GROUP], ctx)
                    turn_ps = ps(f"{pre}_turn", [F, GROUP], ctx)
                    msgT_ps = ps(f"{pre}_msgTps", [F, GROUP], ctx)
                    msgT = sb(f"{pre}_msgT", [F, GROUP], F32, ctx)
                    msg = ps(f"{pre}_msgps", [P, TILES * F], ctx)
                    hT = sb(f"{pre}_hT", [P, DEPTH, GROUP], F32, ctx)
                    split = sb(f"{pre}_split", [P, DEPTH, TYPES // 2, GROUP], F32, ctx)
                if kind == "attention":
                    turn_ps = ps(f"{pre}_turn", [F, GROUP], ctx)
                    proj_ps = ps(f"{pre}_proj", [P, TILES, 2 * HEADS * F], ctx)
                    hT = sb(f"{pre}_hT", [F, DEPTH, GROUP], F32, ctx)
                    msg = sb(f"{pre}_msg", [P, TILES * F], F32, ctx)
                    prod = sb(f"{pre}_prod", [P, TILES, HEADS, F], F32, ctx)
                    score = sb(f"{pre}_score", [P, TILES, HEADS], F32, ctx)
                    top = sb(f"{pre}_top", [P, TILES], F32, ctx)
                    below = sb(f"{pre}_below", [P, TILES, HEADS], F32, ctx)
                    ex = sb(f"{pre}_ex", [P, TILES, HEADS], F32, ctx)
                    exs = sb(f"{pre}_exs", [P, TILES], F32, ctx)
                    rex = sb(f"{pre}_rex", [P, TILES], F32, ctx)
                    attn = sb(f"{pre}_attn", [P, TILES, HEADS], F32, ctx)
                freed = {None: [rest_left], "types": [turned], "attention": [turned, att[0]]}[kind]
                block = ctx.enter_context(nc.Block())

                def group_cols(g):
                    return bass.ds(g * TILES, TILES)

                def whole(slot):
                    if kind is None:
                        return got[0][:, slot, :, :].rearrange("p t f -> p (t f)")
                    return msg[:, :]

                def there(i, q, delta):
                    g = at(i, q, delta)[1]
                    return not isinstance(g, int) or g < GROUPS

                @block.scalar
                def _(act):
                    def stage_group(i, q, delta):
                        slot, g, uses = at(i, q, delta)
                        if given((uses - 1) * 16 * TILES * NG):
                            act.wait_ge(gathered[slot].sem, gathered[slot].base + (uses - 1) * 16 * TILES * NG)
                        if given(g - DEPTH + 1):
                            act.wait_ge(matched.sem, matched.base + g - DEPTH + 1)
                        if find_into:
                            if given(g - DEPTH + 1):
                                act.wait_ge(into_known.sem, into_known.base + g - DEPTH + 1)
                        gate(act)
                        for k, (_, rows, scale, offset) in enumerate(gathers):
                            act.activation(stage[:, slot, k, :], rows[:, group_cols(g)], ACT.Copy, scale=scale, bias=offset)
                        if kind == "types":
                            act.activation(types[:, slot, :], type_f[:, group_cols(g)], ACT.Copy)
                        act.activation(keys[:, slot, :], key[:, group_cols(g)], ACT.Copy).then_inc(rows_staged.sem, 1)

                    def copy_turned(i, q, delta):
                        slot, g, _ = at(i, q, delta)
                        act.wait_ge(turned.sem, turned.base + g + 1)
                        used = {"types": by_type, "attention": projected}[kind]
                        if given(g - DEPTH + 1):
                            act.wait_ge(used.sem, used.base + g - DEPTH + 1)
                        if kind == "types":
                            act.activation(hT[F:P, slot, :], turn_ps[:, :], ACT.Copy)
                        act.activation(hT[0:F, slot, :], turn_ps[:, :], ACT.Copy).then_inc(turned_copied.sem, 1)

                    def copy_messages(i, q, delta):
                        _, g, _ = at(i, q, delta)
                        act.wait_ge(messages_turned.sem, messages_turned.base + g + 1)
                        if given(g):
                            act.wait_ge(messages.sem, messages.base + g)
                        act.activation(msgT[:, :], msgT_ps[:, :], ACT.Copy).then_inc(messages_copied.sem, 1)

                    def first_two_parts(i, q, delta):
                        slot, g, uses = at(i, q, delta)
                        if kind is None:
                            act.wait_ge(gathered[slot].sem, gathered[slot].base + uses * 16 * TILES * NG)
                        else:
                            act.wait_ge(messages.sem, messages.base + g + 1)
                        if given(g - DEPTH + 1):
                            act.wait_ge(summed.sem, summed.base + g - DEPTH + 1)
                        gate(act)
                        act.activation(parts[:, slot, 0, :], whole(slot), ACT.Copy).then_inc(first_part.sem, 1)
                        act.wait_ge(rest_left.sem, rest_left.base + g + 1)
                        act.activation(parts[:, slot, 1, :], rest[:, :], ACT.Copy).then_inc(second_part.sem, 1)

                    def body(i, q):
                        slot, g, uses = at(i, q)
                        if there(i, q, AHEAD + 1):
                            stage_group(i, q, AHEAD + 1)
                        if kind == "types":
                            first_two_parts(i, q, 0)
                        if kind == "attention":
                            act.wait_ge(att[2].sem, att[2].base + g + 1)
                            act.activation(ex[:, :, :], below[:, :, :], ACT.Exp).then_inc(att[3].sem, 1)
                        if kind and there(i, q, AHEAD):
                            copy_turned(i, q, AHEAD)
                        if kind is None and there(i, q, 1):
                            first_two_parts(i, q, 1)
                        if kind == "attention":
                            first_two_parts(i, q, 0)
                        if given((uses - 1) * 16 * TILES):
                            act.wait_ge(scattered[slot].sem, scattered[slot].base + (uses - 1) * 16 * TILES)
                        if find_into:
                            act.wait_ge(into_known.sem, into_known.base + g + 1)
                        gate(act)
                        act.activation(into_st[:, slot, :], into[:, group_cols(g)], ACT.Copy, scale=into_scale).then_inc(into_staged.sem, 1)
                        if kind == "types" and there(i, q, 1):
                            copy_messages(i, q, 1)
                        act.wait_ge(summed.sem, summed.base + g + 1)
                        act.activation(sums[:, slot, :], sum_ps[:, :], ACT.Copy).then_inc(sums_copied.sem, 1)

                    stage_group(0, 0, 0)
                    stage_group(0, 0, 1)
                    if kind:
                        copy_turned(0, 0, 0)
                    if kind == "types":
                        stage_group(0, 0, 2)
                        copy_messages(0, 0, 0)
                        copy_turned(0, 0, 1)
                    if kind is None:
                        first_two_parts(0, 0, 0)
                    rounds(act, body, GROUPS)

                @block.gpsimd
                def _(pool):
                    def gather(i, q):
                        slot, g, uses = at(i, q)
                        pool.wait_ge(rows_staged.sem, rows_staged.base + g + 1)
                        for s in freed:
                            if given(g - DEPTH + 1):
                                pool.wait_ge(s.sem, s.base + g - DEPTH + 1)
                        gate(pool)
                        for k, (rows_of, _, _, _) in enumerate(gathers):
                            for t in range(TILES):
                                pool.indirect_dma_start(out=got[k][:, slot, t, :], out_offset=None, in_=rows_of,
                                                        in_offset=bass.IndirectOffsetOnAxis(ap=stage[:, slot, k, t:t + 1].bitcast(U32), axis=0)
                                                        ).then_inc(gathered[slot].sem, 16)

                    def scatter(i, q):
                        slot, g, _ = at(i, q)
                        before, _, uses = at(i, q, -1)
                        pool.wait_ge(sums_copied.sem, sums_copied.base + g + 1)
                        pool.wait_ge(into_staged.sem, into_staged.base + g + 1)
                        if given(uses * 16 * TILES):
                            pool.wait_ge(scattered[before].sem, scattered[before].base + uses * 16 * TILES)
                        gate(pool)
                        for t in range(TILES):
                            pool.indirect_dma_start(out=table, out_offset=bass.IndirectOffsetOnAxis(ap=into_st[:, slot, t:t + 1].bitcast(U32), axis=0),
                                                    in_=sums[:, slot, t * F:(t + 1) * F], in_offset=None,
                                                    compute_op=ALU.add).then_inc(scattered[slot].sem, 16)

                    def body(i, q):
                        gather(i, q)
                        if not isinstance(i, int) or DEPTH * i + q >= LAG:
                            scatter(i + (q - LAG) // DEPTH, (q - LAG) % DEPTH)

                    rounds(pool, body, GROUPS)
                    R = GROUPS // DEPTH
                    for q in range(DEPTH - LAG, DEPTH):
                        scatter(R - 1, q)
                    for slot in range(DEPTH):
                        pool.wait_ge(scattered[slot].sem, scattered[slot].base + R * 16 * TILES)

                @block.tensor
                def _(pe):
                    def spread_keys(i, q, delta):
                        slot, g, _ = at(i, q, delta)
                        pe.wait_ge(rows_staged.sem, rows_staged.base + g + 1)
                        if given(g):
                            pe.wait_ge(matched.sem, matched.base + g)
                        for t in range(TILES):
                            last = pe.transpose(rows_ps[:, t * P:(t + 1) * P], keys[:, slot, t:t + 1].to_broadcast([P, P]), ident[:, :])
                        last.then_inc(keys_spread.sem, 1)

                    def turn_rows(i, q, delta):
                        slot, g, uses = at(i, q, delta)
                        pe.wait_ge(gathered[slot].sem, gathered[slot].base + uses * 16 * TILES * NG)
                        if given(g):
                            pe.wait_ge(turned_copied.sem, turned_copied.base + g)
                        gate(pe)
                        for t in range(TILES):
                            last = pe.transpose(turn_ps[:, t * P:(t + 1) * P], got[0][:, slot, t, :], ident[:, :])
                        last.then_inc(turned.sem, 1)

                    def spread_types(i, q, delta):
                        slot, g, _ = at(i, q, delta)
                        if given(g):
                            pe.wait_ge(by_type.sem, by_type.base + g)
                        for t in range(TILES):
                            last = pe.matmul(type_ps[:, t * P:(t + 1) * P], types[:, slot, t:t + 1].to_broadcast([P, P]), ident_b[:, :],
                                             start=True, stop=True)
                        last.then_inc(types_spread.sem, 1)

                    def type_messages(i, q, delta):
                        slot, g, _ = at(i, q, delta)
                        pe.wait_ge(by_type.sem, by_type.base + g + 1)
                        if given(g):
                            pe.wait_ge(messages_copied.sem, messages_copied.base + g)
                        for c in range(TYPES // 2):
                            last = pe.matmul(msgT_ps[:, :], type_w[:, c, :], split[:, slot, c, :], start=c == 0, stop=c == TYPES // 2 - 1)
                        last.then_inc(messages_turned.sem, 1)

                    def turn_messages(i, q):
                        _, g, _ = at(i, q)
                        pe.wait_ge(messages_copied.sem, messages_copied.base + g + 1)
                        if given(g):
                            pe.wait_ge(rest_left.sem, rest_left.base + g)
                        gate(pe)
                        for t in range(TILES):
                            last = pe.transpose(msg[:, t * F:(t + 1) * F], msgT[:, t * P:(t + 1) * P], ident[0:F, 0:F])
                        last.then_inc(messages.sem, 1)

                    def project(i, q, delta):
                        slot, g, _ = at(i, q, delta)
                        pe.wait_ge(turned_copied.sem, turned_copied.base + g + 1)
                        if given(g):
                            pe.wait_ge(att[6].sem, att[6].base + g)
                        for t in range(TILES):
                            last = pe.matmul(proj_ps[:, t, :], hT[:, slot, t * P:(t + 1) * P], att_w[:, :], start=True, stop=True)
                        last.then_inc(projected.sem, 1)

                    def sum_targets(i, q):
                        slot, g, _ = at(i, q)
                        pe.wait_ge(parts_made.sem, parts_made.base + g + 1)
                        pe.wait_ge(matched.sem, matched.base + g + 1)
                        if given(g):
                            pe.wait_ge(sums_copied.sem, sums_copied.base + g)
                        for b in range(TILES):
                            for a in range(TILES):
                                for k in range(3):
                                    last = pe.matmul(sum_ps[:, b * F:(b + 1) * F], match[:, slot, a, b * P:(b + 1) * P], parts[:, slot, k, a * F:(a + 1) * F],
                                                     start=a == 0 and k == 0, stop=a == TILES - 1 and k == 2)
                        last.then_inc(summed.sem, 1)

                    def count_earlier(i, q, delta):
                        slot, g, _ = at(i, q, delta)
                        pe.wait_ge(diagonal.sem, diagonal.base + g + 1)
                        if given(g):
                            pe.wait_ge(chosen.sem, chosen.base + g)
                        for b in range(TILES):
                            for a in range(b):
                                pe.matmul(count_ps[:, b:b + 1], match[:, slot, a, b * P:(b + 1) * P], ones[:, :], start=a == 0, stop=False)
                            last = pe.matmul(count_ps[:, b:b + 1], diag[:, b, :], ones[:, :], start=b == 0, stop=True)
                        last.then_inc(counted.sem, 1)

                    def prepare(i, q, delta):
                        if kind == "types":
                            spread_types(i, q, delta)
                        if kind:
                            turn_rows(i, q, delta)
                        if kind == "attention":
                            project(i, q, delta)

                    def body(i, q):
                        ahead = there(i, q, AHEAD)
                        if kind == "types":
                            turn_messages(i, q)
                        if ahead:
                            spread_keys(i, q, AHEAD)
                            prepare(i, q, AHEAD)
                        if kind != "types":
                            sum_targets(i, q)
                        elif there(i, q, 1):
                            type_messages(i, q, 1)
                        if ahead and find_into:
                            count_earlier(i, q, AHEAD)
                        if kind == "types":
                            sum_targets(i, q)

                    spread_keys(0, 0, 0)
                    prepare(0, 0, 0)
                    if find_into:
                        count_earlier(0, 0, 0)
                    if kind == "types":
                        type_messages(0, 0, 0)
                        spread_keys(0, 0, 1)
                        prepare(0, 0, 1)
                        count_earlier(0, 0, 1)
                    rounds(pe, body, GROUPS)

                @block.vector
                def _(dve):
                    def match_group(i, q, delta):
                        slot, g, _ = at(i, q, delta)
                        dve.wait_ge(keys_spread.sem, keys_spread.base + g + 1)
                        if given(g - DEPTH + 1):
                            dve.wait_ge(summed.sem, summed.base + g - DEPTH + 1)
                        for a in range(TILES):
                            last = dve.tensor_scalar(match[:, slot, a, :], rows_ps[:, :], keys[:, slot, a:a + 1], None, ALU.is_equal)
                        last.then_inc(matched.sem, 1)
                        if not find_into:
                            return
                        dve.wait_ge(matched.sem, matched.base + g + 1)
                        if given(g):
                            dve.wait_ge(counted.sem, counted.base + g)
                        dve.tensor_tensor(diag[:, :, :], match[:, slot, :, :].rearrange("p a (b c) -> p (a b) c", c=P)[:, 0:TILES * TILES:TILES + 1, :],
                                          earlier[:, :].unsqueeze(1).to_broadcast([P, TILES, P]), ALU.mult).then_inc(diagonal.sem, 1)

                    def choose_rows(i, q, delta):
                        slot, g, _ = at(i, q, delta)
                        if given(g):
                            dve.wait_ge(chosen.sem, chosen.base + g)
                        dve.tensor_tensor(gap[:, :], spare[:, :], keys[:, slot, :], ALU.subtract).then_inc(spared.sem, 1)
                        dve.wait_ge(counted.sem, counted.base + g + 1)
                        dve.wait_ge(spared.sem, spared.base + g + 1)
                        dve.scalar_tensor_tensor(out=move[:, :], in0=count_ps[:, :], scalar=0.5, in1=gap[:, :], op0=ALU.is_gt, op1=ALU.mult).then_inc(chosen.sem, 1)
                        dve.wait_ge(chosen.sem, chosen.base + g + 1)
                        dve.tensor_tensor(into[:, group_cols(g)], move[:, :], keys[:, slot, :], ALU.add).then_inc(into_known.sem, 1)

                    def split_types(i, q, delta):
                        slot, g, _ = at(i, q, delta)
                        dve.wait_ge(types_spread.sem, types_spread.base + g + 1)
                        dve.wait_ge(turned_copied.sem, turned_copied.base + g + 1)
                        if given(g - DEPTH + 1):
                            dve.wait_ge(messages_turned.sem, messages_turned.base + g - DEPTH + 1)
                        for c in range(TYPES // 2):
                            last = dve.scalar_tensor_tensor(out=split[:, slot, c, :], in0=type_ps[:, :], scalar=type_of[:, c:c + 1], in1=hT[:, slot, :],
                                                            op0=ALU.is_equal, op1=ALU.mult)
                        last.then_inc(by_type.sem, 1)

                    def attend(i, q):
                        slot, g, uses = at(i, q)
                        dve.wait_ge(projected.sem, projected.base + g + 1)
                        dve.wait_ge(gathered[slot].sem, gathered[slot].base + uses * 16 * TILES * NG)
                        if given(g):
                            dve.wait_ge(messages.sem, messages.base + g)
                        by_head = proj_ps[:, :, 0:HEADS * F].rearrange("p t (h f) -> p t h f", h=HEADS)
                        for t in range(TILES):
                            last = dve.tensor_tensor(prod[:, t, :, :], by_head[:, t, :, :], got[1][:, slot, t, :].unsqueeze(1).to_broadcast([P, HEADS, F]), ALU.mult)
                        last.then_inc(att[0].sem, 1)
                        dve.wait_ge(att[0].sem, att[0].base + g + 1)
                        dve.tensor_reduce(score[:, :, :], prod[:, :, :, :], AX.X, ALU.add).then_inc(att[1].sem, 1)
                        dve.wait_ge(att[1].sem, att[1].base + g + 1)
                        dve.tensor_reduce(top[:, :], score[:, :, :], AX.X, ALU.max).then_inc(att[4].sem, 1)
                        dve.wait_ge(att[4].sem, att[4].base + 3 * g + 1)
                        dve.tensor_tensor(below[:, :, :], score[:, :, :], top[:, :].unsqueeze(2).to_broadcast([P, TILES, HEADS]), ALU.subtract).then_inc(att[2].sem, 1)
                        dve.wait_ge(att[3].sem, att[3].base + g + 1)
                        dve.tensor_reduce(exs[:, :], ex[:, :, :], AX.X, ALU.add).then_inc(att[4].sem, 1)
                        dve.wait_ge(att[4].sem, att[4].base + 3 * g + 2)
                        dve.reciprocal(rex[:, :], exs[:, :]).then_inc(att[4].sem, 1)
                        if given(3 * g + 3):
                            dve.wait_ge(att[4].sem, att[4].base + 3 * g + 3)
                        dve.tensor_tensor(attn[:, :, :], ex[:, :, :], rex[:, :].unsqueeze(2).to_broadcast([P, TILES, HEADS]), ALU.mult).then_inc(att[5].sem, 1)
                        dve.wait_ge(att[5].sem, att[5].base + g + 1)
                        values = proj_ps[:, :, HEADS * F:2 * HEADS * F].rearrange("p t (h f) -> p t h f", h=HEADS)
                        for t in range(TILES):
                            last = dve.tensor_tensor(prod[:, t, :, :], values[:, t, :, :], attn[:, t, :].unsqueeze(2).to_broadcast([P, HEADS, F]), ALU.mult)
                        last.then_inc(att[6].sem, 1)
                        dve.wait_ge(att[6].sem, att[6].base + g + 1)
                        if given(g):
                            dve.wait_ge(rest_left.sem, rest_left.base + g)
                        dve.tensor_reduce(msg[:, :].rearrange("p (t f) -> p t f", f=F), prod[:, :, :, :].rearrange("p t h f -> p t f h"), AX.X, ALU.add).then_inc(messages.sem, 1)

                    def leave_rest(i, q, delta):
                        slot, g, _ = at(i, q, delta)
                        dve.wait_ge(first_part.sem, first_part.base + g + 1)
                        if given(g):
                            dve.wait_ge(parts_made.sem, parts_made.base + g)
                        dve.tensor_tensor(rest[:, :], whole(slot), parts[:, slot, 0, :], ALU.subtract).then_inc(rest_left.sem, 1)

                    def third_part(i, q, delta):
                        slot, g, _ = at(i, q, delta)
                        dve.wait_ge(second_part.sem, second_part.base + g + 1)
                        dve.tensor_tensor(parts[:, slot, 2, :], rest[:, :], parts[:, slot, 1, :], ALU.subtract).then_inc(parts_made.sem, 1)

                    def body(i, q):
                        ahead = there(i, q, AHEAD)
                        if find_into and there(i, q, AHEAD - 1):
                            choose_rows(i, q, AHEAD - 1)
                        if kind is None:
                            if ahead:
                                leave_rest(i, q, 1)
                                match_group(i, q, 1)
                                third_part(i, q, 1)
                            return
                        if kind == "attention":
                            attend(i, q)
                        else:
                            leave_rest(i, q, 0)
                        if ahead:
                            match_group(i, q, AHEAD)
                        if kind == "attention":
                            leave_rest(i, q, 0)
                        third_part(i, q, 0)
                        if kind == "types" and ahead:
                            split_types(i, q, AHEAD)

                    match_group(0, 0, 0)
                    if kind is None:
                        leave_rest(0, 0, 0)
                        third_part(0, 0, 0)
                    if kind == "types":
                        split_types(0, 0, 0)
                        choose_rows(0, 0, 0)
                        match_group(0, 0, 1)
                        split_types(0, 0, 1)
                    rounds(dve, body, GROUPS)

            R = GROUPS // DEPTH
            totals = [(s, R * 16 * TILES * NG) for s in gathered] + [(s, R * 16 * TILES) for s in scattered]
            totals += [(s, GROUPS) for s in (rows_staged, keys_spread, matched, into_staged, summed, sums_copied,
                                             first_part, rest_left, second_part, parts_made)]
            if find_into:
                totals += [(s, GROUPS) for s in (diagonal, counted, spared, chosen, into_known)]
            if kind:
                totals += [(s, GROUPS) for s in (turned, turned_copied, messages)]
            if kind == "types":
                totals += [(s, GROUPS) for s in (types_spread, by_type, messages_turned, messages_copied)]
            if kind == "attention":
                totals += [(s, GROUPS) for s in (projected, att[0], att[1], att[2], att[3], att[5], att[6])] + [(att[4], 3 * GROUPS)]
            advance(totals)

        edge_phase("e0", [(t0, dst_row, 1.0, 0.0)], src_key, src_into, 1.0, acc0, True, None)

        with ExitStack() as ctx:
            x_in = sb("p1_x", [P, DEPTH, SLOTS * F], F32, ctx)
            a_in = sb("p1_a", [P, DEPTH, SLOTS * F], F32, ctx)
            x_out = sb("p1_xo", [P, DEPTH, SLOTS * F], F32, ctx)
            mh_out = sb("p1_mh", [P, DEPTH, SLOTS * 2 * F], F32, ctx)
            scaled = sb("p1_sc", [P, 2, HALF, F], F32, ctx)
            norm = Norm(0, ctx, "p1")
            block = ctx.enter_context(nc.Block())

            @block.sync
            def _(sp):
                node_streams(sp, [(x, x_in), (acc0, a_in)], [(x1, x_out), (mh1, mh_out)], x_new, h_new)

            @block.gpsimd
            def _(pool):
                def body(i, q):
                    slot, b, uses = at(i, q)
                    for s in range(2):
                        pool.wait_ge(loaded[slot].sem, loaded[slot].base + 2 * 16 * uses)
                        if given(2 * b + s - 1):
                            pool.wait_ge(x_new.sem, x_new.base + 2 * b + s - 1)
                        gate(pool)
                        pool.tensor_tensor(scaled[:, s, :, :], half(a_in, slot, s), spread(dinv[:, cols(i, q, s)]), ALU.mult).then_inc(mixed.sem, 1)

                rounds(pool, body, BATCHES)

            @block.vector
            def _(dve):
                def new_x(i, q):
                    slot, b, _ = at(i, q)
                    stored_before(dve, i, q, 2)
                    for s in range(2):
                        dve.wait_ge(mixed.sem, mixed.base + 2 * b + s + 1)
                        dve.tensor_tensor(half(x_out, slot, s), half(x_in, slot, s), scaled[:, s, :, :], ALU.add).then_inc(x_new.sem, 1)

                def moments(i, q):
                    slot, b, _ = at(i, q)
                    for s in range(2):
                        dve.wait_ge(x_new.sem, x_new.base + 2 * b + s + 1)
                        norm.dve_sum(dve, 2 * b + s, s, half(x_out, slot, s))
                    for s in range(2):
                        norm.dve_centre(dve, 2 * b + s, s, half(x_out, slot, s))
                    for s in range(2):
                        norm.dve_var(dve, 2 * b + s, s)

                def new_h(i, q):
                    slot, b, _ = at(i, q)
                    for s in range(2):
                        norm.dve_rstd(dve, 2 * b + s, s)
                    for s in range(2):
                        o = halves(mh_out[:, slot, s * HALF * 2 * F:(s + 1) * HALF * 2 * F], 2 * F)[:, :, F:2 * F]
                        norm.dve_relu(dve, 2 * b + s, s, o).then_inc(h_new.sem, 1)

                def body(i, q):
                    first = isinstance(i, int) and i == 0 and q == 0
                    before = (i + (q - 1) // DEPTH, (q - 1) % DEPTH)
                    if not first:
                        moments(*before)
                    new_x(i, q)
                    if not first:
                        new_h(*before)

                dve.memset(mh_out[:, :, :], 0.0).then_inc(step[0].sem, 1)
                dve.wait_ge(step[0].sem, step[0].base + 1)
                rounds(dve, body, BATCHES)
                moments(BATCHES // DEPTH, 0)
                new_h(BATCHES // DEPTH, 0)

            @block.scalar
            def _(act):
                def body(i, q):
                    _, b, _ = at(i, q)
                    for s in range(2):
                        norm.act_square(act, 2 * b + s, s)
                    for s in range(2):
                        norm.act_std(act, 2 * b + s, s)

                rounds(act, body, BATCHES)

            advance(node_signals(2, 2) + norm.totals() + [(s, 2 * BATCHES) for s in (mixed, x_new, h_new)] + [(step[0], 1)])

        edge_phase("e1", [(mh1_rows, src_row, 2.0, 1.0)], dst_key, dst_into, 2.0, mh1_rows, True, "types")

        QUAD = 4
        with ExitStack() as ctx:
            x_in = sb("p2_x", [P, DEPTH, SLOTS * F], F32, ctx)
            mh_in = sb("p2_mh", [P, DEPTH, SLOTS * 2 * F], F32, ctx)
            x_out = sb("p2_xo", [P, DEPTH, SLOTS * F], F32, ctx)
            h_out = sb("p2_ho", [P, DEPTH, SLOTS * F], F32, ctx)
            mhT = sb("p2_mhT", [P, 2, QUAD * P], F32, ctx)
            rz = sb("p2_rz", [P, 2, SLOTS, 2 * F], F32, ctx)
            cand = sb("p2_cand", [P, 2, SLOTS, F], F32, ctx)
            blend = sb("p2_blend", [P, 2, SLOTS, F], F32, ctx)
            turn_ps = [ps(f"p2_turn{k}", [P, QUAD * P], ctx) for k in range(2)]
            gate_ps = [ps(f"p2_gate{k}", [P, QUAD, 4 * F], ctx) for k in range(2)]
            norm = Norm(0, ctx, "p2")
            rz_done, reset_done, cand_in, cand_done, diff_done, blended = step
            keep = mixed
            block = ctx.enter_context(nc.Block())

            def mh_half(slot, s):
                return halves(mh_in[:, slot, s * HALF * 2 * F:(s + 1) * HALF * 2 * F], 2 * F)

            @block.sync
            def _(sp):
                node_streams(sp, [(x1, x_in), (mh1, mh_in)], [(x2, x_out), (h2, h_out), (acc2, h_out)], keep, h_new)

            @block.tensor
            def _(pe):
                def turn_quad(i, q, t):
                    slot, b, uses = at(i, q)
                    m = 4 * b + t
                    pe.wait_ge(loaded[slot].sem, loaded[slot].base + 2 * 16 * uses)
                    if given(m - 1):
                        pe.wait_ge(node_copied.sem, node_copied.base + m - 1)
                    for k in range(QUAD):
                        c = (t * QUAD + k) * P
                        last = pe.transpose(turn_ps[t % 2][:, k * P:(k + 1) * P], mh_in[:, slot, c:c + P], ident[:, :])
                    last.then_inc(node_turned.sem, 1)

                def body(i, q):
                    _, b, _ = at(i, q)
                    turn_quad(i, q, 0)
                    for t in range(4):
                        m = 4 * b + t
                        if t < 3:
                            turn_quad(i, q, t + 1)
                        pe.wait_ge(node_copied.sem, node_copied.base + m + 1)
                        if given(m - 1):
                            pe.wait_ge(rz_done.sem, rz_done.base + m - 1)
                        if given(m - 1):
                            pe.wait_ge(cand_in.sem, cand_in.base + m - 1)
                        for j in range(2):
                            two = gate_ps[t % 2][:, 2 * j:2 * j + 2, :].rearrange("p k f -> p (k f)")
                            pe.matmul(two, ones3[:, :], gate_b_parts[:, :], start=True, stop=False, skip_group_check=True)
                            for k in (2 * j, 2 * j + 1):
                                last = pe.matmul(gate_ps[t % 2][:, k, :], mhT[:, t % 2, k * P:(k + 1) * P], gate_w[:, :],
                                                 start=False, stop=k % 2 == 1, skip_group_check=True)
                        last.then_inc(node_out.sem, 1)

                rounds(pe, body, BATCHES)

            def ring2(b, q):
                return q

            @block.scalar
            def _(act):
                def copy_quad(b, t):
                    m = 4 * b + t
                    act.wait_ge(node_turned.sem, node_turned.base + m + 1)
                    if given(m - 1):
                        act.wait_ge(node_out.sem, node_out.base + m - 1)
                    act.activation(mhT[:, t % 2, :], turn_ps[t % 2][:, :], ACT.Copy).then_inc(node_copied.sem, 1)

                def sigmoid_quad(b, t):
                    m = 4 * b + t
                    act.wait_ge(node_out.sem, node_out.base + m + 1)
                    if t == 0:
                        if given(2 * (b - 1) + 2):
                            act.wait_ge(blended.sem, blended.base + 2 * (b - 1) + 2)
                    act.activation(rz[:, 0, t * QUAD:(t + 1) * QUAD, :], gate_ps[t % 2][:, :, 0:2 * F], ACT.Sigmoid).then_inc(rz_done.sem, 1)

                def tanh_half(b, s):
                    act.wait_ge(cand_in.sem, cand_in.base + 4 * b + 2 * s + 2)
                    a = cand[:, 0, s * HALF:(s + 1) * HALF, :]
                    act.activation(a, a, ACT.Tanh).then_inc(cand_done.sem, 1)

                def squares(i, q):
                    for s in range(2):
                        norm.act_square(act, 2 * at(i, q)[1] + s, s)

                def stds(i, q):
                    for s in range(2):
                        norm.act_std(act, 2 * at(i, q)[1] + s, s)

                def body(i, q):
                    _, b, _ = at(i, q)
                    first = isinstance(i, int) and i == 0 and q == 0
                    before = (i + (q - 1) // DEPTH, (q - 1) % DEPTH)
                    copy_quad(b, 0)
                    copy_quad(b, 1)
                    sigmoid_quad(b, 0)
                    copy_quad(b, 2)
                    sigmoid_quad(b, 1)
                    if not first:
                        squares(*before)
                    copy_quad(b, 3)
                    sigmoid_quad(b, 2)
                    tanh_half(b, 0)
                    sigmoid_quad(b, 3)
                    tanh_half(b, 1)
                    if not first:
                        stds(*before)

                rounds(act, body, BATCHES)
                squares(BATCHES // DEPTH, 0)
                stds(BATCHES // DEPTH, 0)

            @block.gpsimd
            def _(pool):
                def body(i, q):
                    slot, b, uses = at(i, q)
                    for s in range(2):
                        n = 2 * b + s
                        z = rz[:, 0, s * HALF:(s + 1) * HALF, F:2 * F]
                        c = cand[:, 0, s * HALF:(s + 1) * HALF, :]
                        o = blend[:, 0, s * HALF:(s + 1) * HALF, :]
                        pool.wait_ge(cand_done.sem, cand_done.base + n + 1)
                        if given(n - 1):
                            pool.wait_ge(x_new.sem, x_new.base + n - 1)
                        pool.tensor_tensor(o, mh_half(slot, s)[:, :, F:2 * F], c, ALU.subtract).then_inc(diff_done.sem, 1)
                        pool.wait_ge(diff_done.sem, diff_done.base + n + 1)
                        pool.tensor_tensor(o, o, z, ALU.mult).then_inc(blended.sem, 1)
                        pool.tensor_tensor(half(x_in, slot, s), half(x_in, slot, s), c, ALU.add).then_inc(keep.sem, 1)

                rounds(pool, body, BATCHES)

            @block.vector
            def _(dve):
                def gates(i, q, t):
                    _, b, _ = at(i, q)
                    for t in (t, t + 1):
                        m = 4 * b + t
                        dve.wait_ge(rz_done.sem, rz_done.base + m + 1)
                        if t % 2 == 0:
                            if given(2 * (b - 1) + t // 2 + 1):
                                dve.wait_ge(keep.sem, keep.base + 2 * (b - 1) + t // 2 + 1)
                        dve.tensor_tensor(cand[:, 0, t * QUAD:(t + 1) * QUAD, :], gate_ps[t % 2][:, :, 3 * F:4 * F],
                                          rz[:, 0, t * QUAD:(t + 1) * QUAD, 0:F], ALU.mult).then_inc(reset_done.sem, 1)
                    for t in (t - 1, t):
                        m = 4 * b + t
                        dve.wait_ge(reset_done.sem, reset_done.base + m + 1)
                        a = cand[:, 0, t * QUAD:(t + 1) * QUAD, :]
                        dve.tensor_tensor(a, gate_ps[t % 2][:, :, 2 * F:3 * F], a, ALU.add).then_inc(cand_in.sem, 1)

                def new_x(i, q):
                    slot, b, _ = at(i, q)
                    stored_before(dve, i, q, 3)
                    for s in range(2):
                        dve.wait_ge(keep.sem, keep.base + 2 * b + s + 1)
                        dve.tensor_tensor(half(x_out, slot, s), blend[:, 0, s * HALF:(s + 1) * HALF, :], half(x_in, slot, s), ALU.add).then_inc(x_new.sem, 1)

                def centre(i, q):
                    slot, b, _ = at(i, q)
                    for s in range(2):
                        dve.wait_ge(x_new.sem, x_new.base + 2 * b + s + 1)
                        norm.dve_sum(dve, 2 * b + s, s, half(x_out, slot, s))
                    for s in range(2):
                        norm.dve_centre(dve, 2 * b + s, s, half(x_out, slot, s))

                def variance(i, q):
                    for s in range(2):
                        norm.dve_var(dve, 2 * at(i, q)[1] + s, s)

                def new_h(i, q):
                    slot, b, _ = at(i, q)
                    for s in range(2):
                        norm.dve_rstd(dve, 2 * b + s, s)
                    for s in range(2):
                        norm.dve_relu(dve, 2 * b + s, s, half(h_out, slot, s)).then_inc(h_new.sem, 1)

                def body(i, q):
                    first = isinstance(i, int) and i == 0 and q == 0
                    before = (i + (q - 1) // DEPTH, (q - 1) % DEPTH)
                    if not first:
                        new_x(*before)
                        centre(*before)
                    gates(i, q, 0)
                    if not first:
                        variance(*before)
                    gates(i, q, 2)
                    if not first:
                        new_h(*before)

                rounds(dve, body, BATCHES)
                for part in (new_x, centre, variance, new_h):
                    part(BATCHES // DEPTH, 0)

            advance(node_signals(2, 3) + norm.totals()
                    + [(s, 4 * BATCHES) for s in (node_turned, node_copied, node_out, rz_done, reset_done, cand_in)]
                    + [(s, 2 * BATCHES) for s in (cand_done, diff_done, blended, keep, x_new, h_new)])

        edge_phase("e2", [(h2, src_row, 1.0, 0.0), (h2, dst_row, 1.0, 0.0)], dst_key, dst_into, 1.0, acc2, False, "attention")

        with ExitStack() as ctx:
            x_in = sb("p3_x", [P, DEPTH, SLOTS * F], F32, ctx)
            a_in = sb("p3_a", [P, DEPTH, SLOTS * F], F32, ctx)
            x_out = sb("p3_xo", [P, DEPTH, SLOTS * F], F32, ctx)
            u_out = sb("p3_u", [P, DEPTH, SLOTS * F], F32, ctx)
            y = sb("p3_y", [P, 2, HALF, F], F32, ctx)
            scale = sb("p3_scale", [P, 2, HALF], F32, ctx)
            norm_a, norm_x = Norm(0, ctx, "p3a"), Norm(1, ctx, "p3x")
            x_beta, normed, gamma_done, scale_done = step[0], step[1], step[2], step[3]
            block = ctx.enter_context(nc.Block())

            def row_of(k):
                return gb_rows[:, k, :].unsqueeze(1).to_broadcast([P, HALF, F])

            @block.sync
            def _(sp):
                node_streams(sp, [(x2, x_in), (acc2, a_in)], [(x3, x_out), (u3, u_out)], x_new, h_new)

            @block.scalar
            def _(act):
                def body(i, q):
                    _, b, _ = at(i, q)
                    for s in range(2):
                        norm_a.act_square(act, 2 * b + s, s)
                    if not (isinstance(i, int) and i == 0 and q == 0):
                        for s in range(2):
                            norm_x.act_square(act, 2 * (b - 1) + s, s)
                    for s in range(2):
                        norm_a.act_std(act, 2 * b + s, s)
                    if not (isinstance(i, int) and i == 0 and q == 0):
                        for s in range(2):
                            norm_x.act_std(act, 2 * (b - 1) + s, s)

                rounds(act, body, BATCHES)
                for s in range(2):
                    norm_x.act_square(act, 2 * (BATCHES - 1) + s, s)
                for s in range(2):
                    norm_x.act_std(act, 2 * (BATCHES - 1) + s, s)

            @block.gpsimd
            def _(pool):
                def body(i, q):
                    slot, b, uses = at(i, q)
                    pool.wait_ge(loaded[slot].sem, loaded[slot].base + 2 * 16 * uses)
                    for s in range(2):
                        pool.tensor_tensor(half(x_in, slot, s), half(x_in, slot, s), row_of(1), ALU.add).then_inc(x_beta.sem, 1)
                    for s in range(2):
                        pool.wait_ge(normed.sem, normed.base + 2 * b + s + 1)
                        pool.tensor_tensor(y[:, s, :, :], y[:, s, :, :], row_of(0), ALU.mult).then_inc(gamma_done.sem, 1)

                rounds(pool, body, BATCHES)

            @block.vector
            def _(dve):
                def second(i, q, part):
                    slot, b, _ = at(i, q)
                    for s in range(2):
                        n = 2 * b + s
                        if part == 0:
                            if s == 0:
                                stored_before(dve, i, q, 2)
                            dve.wait_ge(gamma_done.sem, gamma_done.base + n + 1)
                            dve.wait_ge(x_beta.sem, x_beta.base + n + 1)
                            dve.tensor_tensor(half(x_out, slot, s), half(x_in, slot, s), y[:, s, :, :], ALU.add).then_inc(x_new.sem, 1)
                        elif part == 1:
                            dve.wait_ge(x_new.sem, x_new.base + n + 1)
                            norm_x.dve_sum(dve, n, s, half(x_out, slot, s))
                        elif part == 2:
                            norm_x.dve_centre(dve, n, s, half(x_out, slot, s))
                        elif part == 3:
                            norm_x.dve_var(dve, n, s)
                        elif part == 4:
                            norm_x.dve_rstd(dve, n, s)
                        elif part == 5:
                            dve.wait_ge(norm_x.s[LN_RSTD].sem, norm_x.s[LN_RSTD].base + n + 1)
                            dve.tensor_tensor(scale[:, s, :], norm_x.rstd[:, s, :], inv_s[:, cols(i, q, s)], ALU.mult).then_inc(scale_done.sem, 1)
                        else:
                            norm_x.dve_relu(dve, n, s, half(u_out, slot, s), scale[:, s, :], scale_done).then_inc(h_new.sem, 1)

                def first(i, q, part):
                    slot, b, uses = at(i, q)
                    for s in range(2):
                        n = 2 * b + s
                        if part == 0:
                            dve.wait_ge(loaded[slot].sem, loaded[slot].base + 2 * 16 * uses)
                            norm_a.dve_sum(dve, n, s, half(a_in, slot, s))
                        elif part == 1:
                            norm_a.dve_centre(dve, n, s, half(a_in, slot, s))
                        elif part == 2:
                            norm_a.dve_var(dve, n, s)
                        elif part == 3:
                            norm_a.dve_rstd(dve, n, s)
                        else:
                            dve.wait_ge(norm_a.s[LN_RSTD].sem, norm_a.s[LN_RSTD].base + n + 1)
                            if given(n - 1):
                                dve.wait_ge(x_new.sem, x_new.base + n - 1)
                            dve.tensor_tensor(y[:, s, :, :], norm_a.xc[:, s, :, :], spread(norm_a.rstd[:, s, :]), ALU.mult).then_inc(normed.sem, 1)

                def body(i, q):
                    begun = not (isinstance(i, int) and i == 0 and q == 0)
                    before = (i + (q - 1) // DEPTH, (q - 1) % DEPTH)
                    if begun:
                        second(*before, 0)
                    first(i, q, 0)
                    if begun:
                        second(*before, 1)
                    first(i, q, 1)
                    if begun:
                        second(*before, 2)
                    first(i, q, 2)
                    if begun:
                        second(*before, 3)
                    first(i, q, 3)
                    if begun:
                        second(*before, 4)
                    first(i, q, 4)
                    if begun:
                        second(*before, 5)
                        second(*before, 6)

                rounds(dve, body, BATCHES)
                for part in range(7):
                    second(BATCHES // DEPTH, 0, part)

            advance(node_signals(2, 2) + norm_a.totals() + norm_x.totals()
                    + [(s, 2 * BATCHES) for s in (x_beta, normed, gamma_done, scale_done, x_new, h_new)])

        edge_phase("e3", [(u3, src_row, 1.0, 0.0)], dst_key, dst_into, 1.0, acc3, False, None)

        with ExitStack() as ctx:
            x_in = sb("p4_x", [P, DEPTH, SLOTS * F], F32, ctx)
            u_in = sb("p4_u", [P, DEPTH, SLOTS * F], F32, ctx)
            a_in = sb("p4_a", [P, DEPTH, SLOTS * F], F32, ctx)
            x_out = sb("p4_xo", [P, DEPTH, SLOTS * F], F32, ctx)
            both = sb("p4_both", [P, 2, HALF, 2 * F], F32, ctx)
            own_h = sb("p4_h", [P, 2, HALF, F], F32, ctx)
            own_a = sb("p4_ha", [P, 2, HALF, F], F32, ctx)
            bothT = sb("p4_bT", [P, 2, HALF * P], F32, ctx)
            leaky = sb("p4_leaky", [P, 2, HALF * F], F32, ctx)
            turn_ps = [ps(f"p4_turn{k}", [P, HALF * P], ctx) for k in range(2)]
            lin_ps = [ps(f"p4_lin{k}", [P, HALF * F], ctx) for k in range(2)]
            acc_scaled, h_scaled, left, right, bent, lin_copied = step
            block = ctx.enter_context(nc.Block())

            @block.sync
            def _(sp):
                node_streams(sp, [(x3, x_in), (u3, u_in), (acc3, a_in)], [(out, x_out)], x_new, x_new)

            @block.gpsimd
            def _(pool):
                def body(i, q):
                    slot, b, uses = at(i, q)
                    for s in range(2):
                        n = 2 * b + s
                        pool.wait_ge(loaded[slot].sem, loaded[slot].base + 3 * 16 * uses)
                        if given(n - 1):
                            pool.wait_ge(left.sem, left.base + n - 1)
                        if given(n - 1):
                            pool.wait_ge(node_turned.sem, node_turned.base + n - 1)
                        gate(pool)
                        pool.tensor_tensor(own_a[:, s, :, :], half(a_in, slot, s), spread(inv_s[:, cols(i, q, s)]), ALU.mult).then_inc(acc_scaled.sem, 1)
                        pool.tensor_tensor(both[:, s, :, F:2 * F], half(a_in, slot, s), half(u_in, slot, s), ALU.mult).then_inc(right.sem, 1)

                rounds(pool, body, BATCHES)

            @block.vector
            def _(dve):
                def finish(i, q):
                    slot, b, _ = at(i, q)
                    stored_before(dve, i, q, 1)
                    for s in range(2):
                        dve.wait_ge(lin_copied.sem, lin_copied.base + 2 * b + s + 1)
                        dve.scalar_tensor_tensor(out=leaky[:, s, :], in0=leaky[:, s, :], scalar=LEAKY, in1=leaky[:, s, :],
                                                 op0=ALU.mult, op1=ALU.max).then_inc(bent.sem, 1)
                    for s in range(2):
                        dve.wait_ge(bent.sem, bent.base + 2 * b + s + 1)
                        dve.tensor_tensor(half(x_out, slot, s), half(x_in, slot, s), halves(leaky[:, s, :]), ALU.add).then_inc(x_new.sem, 1)

                def body(i, q):
                    slot, b, uses = at(i, q)
                    dve.wait_ge(loaded[slot].sem, loaded[slot].base + 3 * 16 * uses)
                    for s in range(2):
                        if given(2 * b + s - 1):
                            dve.wait_ge(left.sem, left.base + 2 * b + s - 1)
                        dve.tensor_tensor(own_h[:, s, :, :], half(u_in, slot, s), spread(sqrt_s[:, cols(i, q, s)]), ALU.mult).then_inc(h_scaled.sem, 1)
                    for s in range(2):
                        n = 2 * b + s
                        dve.wait_ge(h_scaled.sem, h_scaled.base + n + 1)
                        dve.wait_ge(acc_scaled.sem, acc_scaled.base + n + 1)
                        if given(n - 1):
                            dve.wait_ge(node_turned.sem, node_turned.base + n - 1)
                        dve.tensor_tensor(both[:, s, :, 0:F], own_h[:, s, :, :], own_a[:, s, :, :], ALU.add).then_inc(left.sem, 1)
                    if not (isinstance(i, int) and i == 0 and q == 0):
                        finish(i + (q - 1) // DEPTH, (q - 1) % DEPTH)

                rounds(dve, body, BATCHES)
                finish(BATCHES // DEPTH, 0)

            @block.tensor
            def _(pe):
                def body(i, q):
                    _, b, _ = at(i, q)
                    for s in range(2):
                        n = 2 * b + s
                        pe.wait_ge(left.sem, left.base + n + 1)
                        pe.wait_ge(right.sem, right.base + n + 1)
                        if given(n - 1):
                            pe.wait_ge(node_copied.sem, node_copied.base + n - 1)
                        for k in range(HALF):
                            last = pe.transpose(turn_ps[s][:, k * P:(k + 1) * P], both[:, s, k, :], ident[:, :])
                        last.then_inc(node_turned.sem, 1)
                    for s in range(2):
                        n = 2 * b + s
                        pe.wait_ge(node_copied.sem, node_copied.base + n + 1)
                        if given(n - 1):
                            pe.wait_ge(lin_copied.sem, lin_copied.base + n - 1)
                        for k in range(HALF):
                            last = pe.matmul(lin_ps[s][:, k * F:(k + 1) * F], bothT[:, s, k * P:(k + 1) * P], w12[:, :], start=True, stop=True)
                        last.then_inc(node_out.sem, 1)

                rounds(pe, body, BATCHES)

            @block.scalar
            def _(act):
                def body(i, q):
                    _, b, _ = at(i, q)
                    for s in range(2):
                        n = 2 * b + s
                        act.wait_ge(node_turned.sem, node_turned.base + n + 1)
                        if given(n - 1):
                            act.wait_ge(node_out.sem, node_out.base + n - 1)
                        act.activation(bothT[:, s, :], turn_ps[s][:, :], ACT.Copy).then_inc(node_copied.sem, 1)
                    for s in range(2):
                        n = 2 * b + s
                        act.wait_ge(node_out.sem, node_out.base + n + 1)
                        if given(n - 1):
                            act.wait_ge(x_new.sem, x_new.base + n - 1)
                        act.activation(leaky[:, s, :], lin_ps[s][:, :], ACT.Copy).then_inc(lin_copied.sem, 1)

                rounds(act, body, BATCHES)


def kernel(x, src, dst, edge_type_8, L0_gnn_W, L0_gnn_b, L1_gnn_edge_matrix, L1_gnn_w_ih, L1_gnn_w_hh,
           L1_gnn_b_ih, L1_gnn_b_hh, L2_gnn_Wq, L2_gnn_Wk, L2_gnn_Wv, L2_gnn_Wo, L2_gnn_gamma,
           L2_gnn_beta, L3_gnn_W1, L3_gnn_W2):
    import numpy as np
    import concourse.bacc as bacc
    from concourse.bass_utils import run_bass_kernel_spmd

    by_type = np.asarray(L1_gnn_edge_matrix).reshape(TYPES, F, F).transpose(0, 2, 1).reshape(TYPES * F, F)
    arrays = {
        "x": x, "src": src, "dst": dst, "edge_type": edge_type_8,
        "w0t": np.asarray(L0_gnn_W).T, "b0": L0_gnn_b, "at_w": by_type,
        "w_iht": np.asarray(L1_gnn_w_ih).T, "w_hht": np.asarray(L1_gnn_w_hh).T,
        "b_ih": L1_gnn_b_ih, "b_hh": L1_gnn_b_hh,
        "wqt": np.asarray(L2_gnn_Wq).T, "wkt": np.asarray(L2_gnn_Wk).T, "wvt": np.asarray(L2_gnn_Wv).T,
        "wo": L2_gnn_Wo, "gamma": L2_gnn_gamma, "beta": L2_gnn_beta, "w1": L3_gnn_W1, "w2": L3_gnn_W2,
    }
    arrays = {f"in_{k}": np.ascontiguousarray(a) for k, a in arrays.items()}
    nc = bacc.Bacc("TRN2", target_bir_lowering=False, num_devices=1)
    args = [nc.dram_tensor(k, a.shape, mybir.dt.from_np(a.dtype), kind="ExternalInput").ap() for k, a in arrays.items()]
    result = nc.dram_tensor("out_x", x.shape, mybir.dt.from_np(np.dtype(x.dtype)), kind="ExternalOutput").ap()
    graph_layers(nc, *args, result)
    r = run_bass_kernel_spmd(nc, [arrays], core_ids=[0])
    return r.results[0]["out_x"]
```

```python
from contextlib import ExitStack

import concourse.bass as bass
from concourse import mybir

F32 = mybir.dt.float32
BF16 = mybir.dt.bfloat16
FP16 = mybir.dt.float16
I32 = mybir.dt.int32
U32 = mybir.dt.uint32
ALU = mybir.AluOpType
ACT = mybir.ActivationFunctionType
AX = mybir.AxisListType

P = 128
F = 64
HEADS = 4
TYPES = 8
DEPTH = 3
TILES = 4
SLOTS = 16
HALF = SLOTS // 2
LEAKY = 0.01
EPS = 1e-5


class Signal:

    def __init__(self, handle):
        self.sem, self.base = handle, 0


def given(value):
    return not isinstance(value, int) or value > 0


def at(i, q, delta=0):
    return (q + delta) % DEPTH, DEPTH * i + (q + delta), i + (q + delta) // DEPTH + 1


def rounds(engine, body, steps, ahead=1):
    last = (steps - ahead) // DEPTH
    for q in range(DEPTH):
        body(0, q)
    with engine.Fori(1, last, 1) as i:
        for q in range(DEPTH):
            body(i, q)
    for n in range(DEPTH * last, steps):
        body(n // DEPTH, n % DEPTH)


def graph_layers(nc, x, src, dst, edge_type, w0t, b0, at_w, w_iht, w_hht, b_ih, b_hh,
                 wqt, wkt, wvt, wo, gamma, beta, w1, w2, out):
    N, E = x.shape[0], src.shape[0]
    BATCH = P * SLOTS
    BATCHES = -(-N // BATCH)
    NP = BATCHES * BATCH
    COLS = BATCHES * SLOTS
    LAST_P = (N - (BATCHES - 1) * BATCH) // SLOTS
    assert (N - (BATCHES - 1) * BATCH) % SLOTS == 0 and BATCHES % DEPTH == 1
    GROUP = TILES * P
    NR = NP + GROUP
    EFULL = E // P
    EREST = E - EFULL * P
    GROUPS = -(-(EFULL + 1) // TILES)
    ECOLS = GROUPS * TILES
    COUNTED = 2 * TILES
    assert ECOLS % COUNTED == 0

    def dram(name, shape):
        return nc.dram_tensor(name, shape, F32, kind="Internal").ap()

    t0 = dram("t0", (NR, F))
    acc0 = dram("acc0", (NR, F))
    x1 = dram("x1", (NP, F))
    mh1 = dram("mh1", (NR, 2 * F))
    x2 = dram("x2", (NP, F))
    h2 = dram("h2", (NR, F))
    acc2 = dram("acc2", (NR, F))
    x3 = dram("x3", (NP, F))
    u3 = dram("u3", (NR, F))
    acc3 = dram("acc3", (NR, F))
    mh1_rows = mh1.rearrange("n (k f) -> (n k) f", k=2)

    whole_kernel = ExitStack()
    with whole_kernel:
        def sb(name, shape, dt=F32, ctx=whole_kernel):
            return ctx.enter_context(nc.sbuf_tensor(name, shape, dt))

        def ps(name, shape, ctx, dt=F32):
            return ctx.enter_context(nc.psum_tensor(name, shape, dt))

        def signal(name):
            return Signal(whole_kernel.enter_context(nc.semaphore(name)))

        def signals(name, n=DEPTH):
            return [signal(f"{name}{k}") for k in range(n)]

        ident = sb("ident", [P, P])
        src_row = sb("src_row", [P, ECOLS], I32)
        dst_row = sb("dst_row", [P, ECOLS], I32)
        src_key = sb("src_key", [P, ECOLS])
        dst_key = sb("dst_key", [P, ECOLS])
        type_f = sb("type_f", [P, ECOLS])
        src_into = sb("src_into", [P, ECOLS], I32)
        dst_into = sb("dst_into", [P, ECOLS], I32)
        spare = sb("spare", [P, TILES])
        earlier = sb("earlier", [P, P], BF16)
        ones = sb("ones", [P, 1], BF16)
        ident_b = sb("ident_b", [P, P], BF16)
        dinv = sb("dinv", [P, COLS])
        inv_s = sb("inv_s", [P, COLS])
        sqrt_s = sb("sqrt_s", [P, COLS])
        w0_pair = sb("w0_pair", [P, P])
        ones3 = sb("ones3", [3, P], BF16)
        b0_parts = sb("b0_parts", [3, 8 * F], BF16)
        gate_w = sb("gate_w", [P, 4 * F])
        gate_b_parts = sb("gate_b_parts", [3, 8 * F], BF16)
        type_w = sb("type_w", [P, TYPES // 2, F])
        type_of = sb("type_of", [P, TYPES // 2])
        att_w = sb("att_w", [F, 2 * HEADS * F])
        gb_rows = sb("gb_rows", [P, 2, F])
        w12 = sb("w12", [P, F])
        eps_t = sb("eps_t", [P, 1])

        rows_staged = signal("rows_staged")
        turn = signal("turn")
        gathered = signals("gathered")
        keys_spread = signal("keys_spread")
        matched = signal("matched")
        diagonal = signal("diagonal")
        counted = signal("counted")
        spared = signal("spared")
        chosen = signal("chosen")
        into_known = signal("into_known")
        into_staged = signal("into_staged")
        summed = signal("summed")
        sums_copied = signal("sums_copied")
        scattered = signals("scattered")
        turned = signal("turned")
        turned_copied = signal("turned_copied")
        types_spread = signal("types_spread")
        by_type = signal("by_type")
        messages_turned = signal("messages_turned")
        messages_copied = signal("messages_copied")
        messages = signal("messages")
        first_part = signal("first_part")
        rest_left = signal("rest_left")
        second_part = signal("second_part")
        parts_made = signal("parts_made")
        projected = signal("projected")
        att = signals("att_step", 7)

        loaded = signals("loaded")
        stored = signals("stored")
        mixed = signal("mixed")
        x_new = signal("x_new")
        ln = [[signal(f"ln{k}_{s}") for s in ("sum", "centred", "squared", "var", "std", "rstd")]
              for k in range(2)]
        h_new = signal("h_new")
        node_turned = signal("node_turned")
        node_copied = signal("node_copied")
        node_out = signal("node_out")
        t_done = signal("t_done")
        step = signals("node_step", 6)

        def advance(counts):
            for s, n in counts:
                s.base += n

        with ExitStack() as ctx:
            raw = sb("raw", [P, 3, ECOLS], I32, ctx)
            hi_i = sb("hi_i", [P, ECOLS], I32, ctx)
            lo_i = sb("lo_i", [P, 2, ECOLS], I32, ctx)
            hi_f = sb("hi_f", [P, ECOLS], F32, ctx)
            lo_f = sb("lo_f", [P, ECOLS], F32, ctx)
            iota_i = sb("iota_i", [P, COLS], I32, ctx)
            iota = sb("iota", [P, COLS], FP16, ctx)
            type_i = sb("type_i", [P, TYPES // 2], I32, ctx)
            type_h = sb("type_h", [P, TYPES // 2], I32, ctx)
            spare_i = sb("spare_i", [P, TILES], I32, ctx)
            hot_p = sb("hot_p", [P, COUNTED, P], BF16, ctx)
            hot_c = sb("hot_c", [P, COUNTED, COLS], BF16, ctx)
            zero = sb("zero", [P, BATCH * F // P], F32, ctx)
            bias = sb("bias", [1, 2, 3 * F], F32, ctx)
            b_gate = sb("b_gate", [1, 4 * F], F32, ctx)
            b_zero = sb("b_zero", [1, F], F32, ctx)
            part = sb("part", [1, 2, 3, 8 * F], BF16, ctx)
            rest = sb("rest", [1, 2, 2, 8 * F], F32, ctx)
            b_rep = sb("b_rep", [1, 2, 8 * F], F32, ctx)
            wq_s = sb("wq_s", [F, HEADS, F], F32, ctx)
            wk_s = sb("wk_s", [F, HEADS, F], F32, ctx)
            wv_s = sb("wv_s", [F, HEADS, F], F32, ctx)
            wo_s = sb("wo_s", [F, HEADS, F], F32, ctx)
            cnt1 = sb("cnt1", [P, COLS], F32, ctx)
            cnt2 = sb("cnt2", [P, COLS], F32, ctx)
            root = [sb(f"root{k}", [P, COLS], F32, ctx) for k in range(2)]
            near = [sb(f"near{k}", [P, COLS], F32, ctx) for k in range(2)]
            error = [sb(f"error{k}", [P, COLS], F32, ctx) for k in range(2)]
            count_ps = [ps(f"count_ps{k}", [P, COLS // 2], ctx) for k in range(2)]
            att_ps = ps("att_ps", [F, 512], ctx)

            def local(name):
                return Signal(ctx.enter_context(nc.semaphore(name)))

            raw_set = local("raw_set")
            raw_in = local("raw_in")
            zero_set = local("zero_set")
            zeroed = local("zeroed")
            w_clear = local("w_clear")
            w_in = local("w_in")
            parts_done = local("parts_done")
            parts_moved = local("parts_moved")
            v_step = local("v_step")
            g_step = local("g_step")
            rest_done = local("rest_done")
            hot = local("hot")
            tile_counted = local("tile_counted")
            att_out = local("att_out")
            rooted = local("rooted")

            block = ctx.enter_context(nc.Block())

            @block.sync
            def _(sp):
                sp.wait_ge(raw_set.sem, raw_set.base + 2)
                for k, a in enumerate((src, dst, edge_type)):
                    sp.dma_start(raw[:, k, 0:EFULL], a[0:P * EFULL].rearrange("(p t) -> p t", t=EFULL)).then_inc(raw_in.sem, 16)
                    sp.dma_start(raw[0:EREST, k, EFULL:EFULL + 1], a[P * EFULL:E].rearrange("(p t) -> p t", t=1)).then_inc(raw_in.sem, 16)
                sp.wait_ge(w_clear.sem, w_clear.base + 2)
                sp.dma_start(w0_pair[0:F, 0:F], w0t).then_inc(w_in.sem, 16)
                sp.dma_start(w0_pair[F:P, F:P], w0t).then_inc(w_in.sem, 16)
                sp.dma_start(gate_w[0:F, 0:3 * F], w_iht).then_inc(w_in.sem, 16)
                sp.dma_start(gate_w[F:P, 0:2 * F], w_hht[:, 0:2 * F]).then_inc(w_in.sem, 16)
                sp.dma_start(gate_w[F:P, 3 * F:4 * F], w_hht[:, 2 * F:3 * F]).then_inc(w_in.sem, 16)
                sp.dma_start(type_w[:, :, :], at_w.rearrange("(c p) m -> p c m", p=P)).then_inc(w_in.sem, 16)
                for s, w in ((wq_s, wqt), (wk_s, wkt), (wv_s, wvt), (wo_s, wo)):
                    sp.dma_start(s[:, :, :], w.rearrange("(h d) j -> d h j", h=HEADS)).then_inc(w_in.sem, 16)
                sp.dma_start(w12[0:F, :], w1).then_inc(w_in.sem, 16)
                sp.dma_start(w12[F:P, :], w2).then_inc(w_in.sem, 16)
                for k, a in enumerate((gamma, beta)):
                    sp.dma_start(gb_rows[:, k, :], a.rearrange("(a f) -> a f", a=1).to_broadcast([P, F])).then_inc(w_in.sem, 16)
                for k, a in enumerate((b_ih, b_hh)):
                    sp.dma_start(bias[0:1, k, :], a.rearrange("(a f) -> a f", a=1)).then_inc(w_in.sem, 16)
                sp.dma_start(b_zero[0:1, :], b0.rearrange("(a f) -> a f", a=1)).then_inc(w_in.sem, 16)
                sp.wait_ge(zero_set.sem, zero_set.base + 1)
                for b in range(BATCHES):
                    sp.dma_start(acc3[b * BATCH:(b + 1) * BATCH, :].rearrange("(p g) f -> p (g f)", p=P), zero[:, :]).then_inc(zeroed.sem, 16)
                for t in (t0, acc0, mh1, h2, acc2, u3, acc3):
                    w = (NR - NP) * t.shape[1] // P
                    sp.dma_start(t[NP:NR, :].rearrange("(p g) f -> p (g f)", p=P), zero[:, 0:w]).then_inc(zeroed.sem, 16)
                sp.wait_ge(parts_done.sem, parts_done.base + 3)
                for k, b in enumerate((b0_parts, gate_b_parts)):
                    for j in range(3):
                        sp.dma_start(b[j:j + 1, :], part[0:1, k, j, :]).then_inc(parts_moved.sem, 16)
                sp.wait_ge(parts_moved.sem, parts_moved.base + 6 * 16)
                sp.wait_ge(zeroed.sem, zeroed.base + (BATCHES + 7) * 16)

            @block.gpsimd
            def _(pool):
                pool.iota(raw[:, 0, :], [[0, ECOLS // TILES], [P, TILES]], base=NP, channel_multiplier=1).then_inc(raw_set.sem, 1)
                pool.iota(raw[:, 1, :], [[0, ECOLS // TILES], [P, TILES]], base=NP, channel_multiplier=1).then_inc(raw_set.sem, 1)
                pool.iota(spare_i[:, :], [[P, TILES]], base=NP, channel_multiplier=1).then_inc(g_step.sem, 1)
                pool.iota(iota_i[:, :], [[1, COLS]], base=0, channel_multiplier=0).then_inc(g_step.sem, 1)
                pool.iota(type_i[:, :], [[P, TYPES // 2]], base=0, channel_multiplier=1).then_inc(g_step.sem, 1)
                pool.memset(ident[:, :], 0.0).then_inc(g_step.sem, 1)
                pool.memset(earlier[:, :], 1.0).then_inc(g_step.sem, 1)
                pool.memset(ident_b[:, :], 0.0).then_inc(g_step.sem, 1)
                pool.wait_ge(g_step.sem, g_step.base + 6)
                pool.affine_select(out=ident_b[:, :], in_=ident_b[:, :], compare_op=ALU.not_equal, fill=1.0,
                                   base=0, pattern=[[-1, P]], channel_multiplier=1).then_inc(g_step.sem, 1)
                pool.affine_select(out=ident[:, :], in_=ident[:, :], compare_op=ALU.not_equal, fill=1.0,
                                   base=0, pattern=[[-1, P]], channel_multiplier=1).then_inc(g_step.sem, 1)
                pool.affine_select(out=earlier[:, :], in_=earlier[:, :], compare_op=ALU.is_gt, fill=0.0,
                                   base=0, pattern=[[1, P]], channel_multiplier=-1).then_inc(g_step.sem, 1)
                pool.memset(eps_t[:, :], EPS)
                pool.memset(ones[:, :], 1.0).then_inc(g_step.sem, 1)
            @block.scalar
            def _(act):
                act.wait_ge(att_out.sem, att_out.base + 1)
                act.activation(att_w[:, 0:HEADS * F], att_ps[:, 0:HEADS * F], ACT.Copy, scale=float(F) ** -0.5)
                act.activation(att_w[:, HEADS * F:2 * HEADS * F], att_ps[:, HEADS * F:2 * HEADS * F], ACT.Copy)
                act.wait_ge(v_step.sem, v_step.base + 12)
                act.activation(root[0][:, :], cnt1[:, :], ACT.Sqrt)
                act.activation(root[1][:, :], cnt2[:, :], ACT.Sqrt).then_inc(rooted.sem, 1)

            @block.tensor
            def _(pe):
                pe.wait_ge(w_in.sem, w_in.base + 17 * 16)
                for h in range(HEADS):
                    pe.matmul(att_ps[:, h * F:(h + 1) * F], wq_s[:, h, :], wk_s[:, h, :], start=True, stop=True)
                for h in range(HEADS):
                    last = pe.matmul(att_ps[:, (HEADS + h) * F:(HEADS + h + 1) * F], wv_s[:, h, :], wo_s[:, h, :], start=True, stop=True)
                last.then_inc(att_out.sem, 1)

                def count(i, k, first, final):
                    pe.wait_ge(hot.sem, hot.base + i * COUNTED + k + 1)
                    for j in range(2):
                        w = COLS // 2
                        last = pe.matmul(count_ps[j][:, :], hot_p[:, k, :], hot_c[:, k, j * w:(j + 1) * w], start=first, stop=final)
                    last.then_inc(tile_counted.sem, 1)

                ROUNDS = ECOLS // COUNTED
                for k in range(COUNTED):
                    count(0, k, k == 0, False)
                with pe.Fori(1, ROUNDS - 1, 1) as i:
                    for k in range(COUNTED):
                        count(i, k, False, False)
                for k in range(COUNTED):
                    count(ROUNDS - 1, k, False, k == COUNTED - 1)

            @block.vector
            def _(dve):
                steps = [0]

                def then(ins):
                    ins.then_inc(v_step.sem, 1)
                    steps[0] += 1

                def after():
                    dve.wait_ge(v_step.sem, v_step.base + steps[0])

                dve.memset(zero[:, :], 0.0).then_inc(zero_set.sem, 1)
                dve.memset(w0_pair[:, :], 0.0).then_inc(w_clear.sem, 1)
                dve.memset(gate_w[:, :], 0.0).then_inc(w_clear.sem, 1)
                dve.memset(ones3[:, :], 1.0)
                dve.wait_ge(raw_in.sem, raw_in.base + 6 * 16)
                dve.wait_ge(g_step.sem, g_step.base + 5)
                slot_bits, part_bits = SLOTS.bit_length() - 1, P.bit_length() - 1
                then(dve.tensor_scalar(hi_i[:, :], raw[:, 0, :], slot_bits, P - 1, ALU.logical_shift_right, ALU.bitwise_and))
                then(dve.tensor_scalar(lo_i[:, 0, :], raw[:, 0, :], slot_bits + part_bits, slot_bits, ALU.logical_shift_right, ALU.logical_shift_left))
                then(dve.tensor_scalar(lo_i[:, 1, :], raw[:, 0, :], SLOTS - 1, None, ALU.bitwise_and))
                after()
                then(dve.tensor_copy(hi_f[:, :], hi_i[:, :]))
                then(dve.tensor_tensor(lo_f[:, :], lo_i[:, 0, :], lo_i[:, 1, :], ALU.add))
                then(dve.tensor_copy(iota[:, :], iota_i[:, :]))
                after()

                def one_hot(i, k):
                    if given((i - 1) * COUNTED + k + 1):
                        dve.wait_ge(tile_counted.sem, tile_counted.base + (i - 1) * COUNTED + k + 1)
                    col = i * COUNTED + k
                    dve.tensor_scalar(hot_p[:, k, :], iota[:, 0:P], hi_f[:, bass.ds(col, 1)], None, ALU.is_equal)
                    dve.tensor_scalar(hot_c[:, k, :], iota[:, :], lo_f[:, bass.ds(col, 1)], None, ALU.is_equal).then_inc(hot.sem, 1)

                for k in range(COUNTED):
                    one_hot(0, k)
                with dve.Fori(1, ECOLS // COUNTED, 1) as i:
                    for k in range(COUNTED):
                        one_hot(i, k)

                dve.tensor_copy(src_key[:, :], raw[:, 0, :])
                dve.tensor_copy(dst_key[:, :], raw[:, 1, :])
                dve.memset(src_row[:, :], 0)
                dve.memset(dst_row[:, :], 0)
                dve.memset(type_f[:, :], 0.0)
                then(dve.tensor_copy(spare[:, :], spare_i[:, :]))
                after()
                for a, k in ((src_row, 0), (dst_row, 1), (type_f, 2)):
                    dve.tensor_copy(a[:, 0:EFULL], raw[:, k, 0:EFULL])
                    dve.tensor_copy(a[0:EREST, EFULL:EFULL + 1], raw[0:EREST, k, EFULL:EFULL + 1])
                dve.memset(src_into[:, :], 0)
                dve.memset(dst_into[:, :], 0)
                then(dve.tensor_scalar(type_h[:, :], type_i[:, :], 6, None, ALU.logical_shift_right))
                dve.wait_ge(w_in.sem, w_in.base + 17 * 16)
                dve.tensor_tensor(b_gate[0:1, 0:2 * F], bias[0:1, 0, 0:2 * F], bias[0:1, 1, 0:2 * F], ALU.add)
                dve.tensor_copy(b_gate[0:1, 2 * F:3 * F], bias[0:1, 0, 2 * F:3 * F])
                then(dve.tensor_copy(b_gate[0:1, 3 * F:4 * F], bias[0:1, 1, 2 * F:3 * F]))
                after()
                dve.tensor_copy(type_of[:, :], type_h[:, :])
                dve.tensor_copy(b_rep[0:1, 0, :].rearrange("p (r f) -> p r f", r=8), b_zero[0:1, :].unsqueeze(1).to_broadcast([1, 8, F]))
                then(dve.tensor_copy(b_rep[0:1, 1, :].rearrange("p (r f) -> p r f", r=2), b_gate[0:1, :].unsqueeze(1).to_broadcast([1, 2, 4 * F])))
                after()
                dve.tensor_copy(part[0:1, :, 0, :], b_rep[0:1, :, :]).then_inc(parts_done.sem, 1)
                dve.wait_ge(parts_done.sem, parts_done.base + 1)
                then(dve.tensor_tensor(rest[0:1, 0, :, :], b_rep[0:1, :, :], part[0:1, :, 0, :], ALU.subtract))
                after()
                dve.tensor_copy(part[0:1, :, 1, :], rest[0:1, 0, :, :]).then_inc(parts_done.sem, 1)
                dve.wait_ge(parts_done.sem, parts_done.base + 2)
                dve.tensor_tensor(rest[0:1, 1, :, :], rest[0:1, 0, :, :], part[0:1, :, 1, :], ALU.subtract).then_inc(rest_done.sem, 1)
                dve.wait_ge(rest_done.sem, rest_done.base + 1)
                dve.tensor_copy(part[0:1, :, 2, :], rest[0:1, 1, :, :]).then_inc(parts_done.sem, 1)
                dve.wait_ge(tile_counted.sem, tile_counted.base + ECOLS)
                for j in range(2):
                    w = COLS // 2
                    dve.tensor_scalar(cnt1[:, j * w:(j + 1) * w], count_ps[j][:, :], 1.0, None, ALU.add)
                    last = dve.tensor_scalar(cnt2[:, j * w:(j + 1) * w], count_ps[j][:, :], 1.0, None, ALU.max)
                then(last)
                dve.wait_ge(rooted.sem, rooted.base + 1)
                dve.reciprocal(near[0][:, :], root[0][:, :])
                then(dve.reciprocal(near[1][:, :], root[1][:, :]))
                after()
                dve.tensor_tensor(error[0][:, :], cnt1[:, :], near[0][:, :], ALU.mult)
                then(dve.tensor_tensor(error[1][:, :], cnt2[:, :], near[1][:, :], ALU.mult))
                for k in range(2):
                    after()
                    then(dve.tensor_tensor(error[k][:, :], error[k][:, :], near[k][:, :], ALU.mult))
                after()
                dve.tensor_scalar(error[0][:, :], error[0][:, :], -0.5, 1.5, ALU.mult, ALU.add)
                then(dve.tensor_scalar(error[1][:, :], error[1][:, :], -0.5, 1.5, ALU.mult, ALU.add))
                after()
                dve.tensor_tensor(dinv[:, :], error[0][:, :], near[0][:, :], ALU.mult)
                then(dve.tensor_tensor(inv_s[:, :], error[1][:, :], near[1][:, :], ALU.mult))
                after()
                dve.tensor_tensor(sqrt_s[:, :], cnt2[:, :], inv_s[:, :], ALU.mult)

        def batch(t, b):
            return t[bass.ds(b * BATCH, BATCH), :].rearrange("(p g) f -> p (g f)", p=P)

        def last_batch(t):
            return t[(BATCHES - 1) * BATCH:N, :].rearrange("(p g) f -> p (g f)", g=SLOTS)

        def halves(a, width=F):
            return a.rearrange("p (g f) -> p g f", f=width)

        def node_streams(sp, loads, stores, freed, done, behind=2):
            def load(i, q):
                slot, b, _ = at(i, q)
                if given(2 * (b - DEPTH) + 2):
                    sp.wait_ge(freed.sem, freed.base + 2 * (b - DEPTH) + 2)
                for table, tile in loads:
                    if isinstance(b, int) and b == BATCHES - 1 and table.shape[0] == N:
                        sp.dma_start(tile[0:LAST_P, slot, :], last_batch(table)).then_inc(loaded[slot].sem, 16)
                    else:
                        sp.dma_start(tile[:, slot, :], batch(table, b)).then_inc(loaded[slot].sem, 16)

            def store(i, q):
                slot, b, _ = at(i, q)
                sp.wait_ge(done.sem, done.base + 2 * b + 2)
                for table, tile in stores:
                    if isinstance(b, int) and b == BATCHES - 1 and table.shape[0] == N:
                        sp.dma_start(last_batch(table), tile[0:LAST_P, slot, :]).then_inc(stored[slot].sem, 16)
                    else:
                        sp.dma_start(batch(table, b), tile[:, slot, :]).then_inc(stored[slot].sem, 16)

            def body(i, q):
                load(i + (q + 1) // DEPTH, (q + 1) % DEPTH)
                if not isinstance(i, int) or DEPTH * i + q >= behind:
                    store(i + (q - behind) // DEPTH, (q - behind) % DEPTH)

            R = BATCHES // DEPTH
            load(0, 0)
            for q in range(DEPTH):
                body(0, q)
            with sp.Fori(1, R - 1, 1) as i:
                for q in range(DEPTH):
                    body(i, q)
            for q in range(DEPTH):
                body(R - 1, q)
            for q in range(DEPTH - behind, DEPTH):
                store(R - 1, q)
            store(R, 0)
            for slot in range(DEPTH):
                sp.wait_ge(stored[slot].sem, stored[slot].base + 16 * len(stores) * (R + (slot == 0)))

        def stored_before(engine, i, q, n_stores):
            slot, _, uses = at(i, q, -DEPTH)
            if given(uses * 16 * n_stores):
                engine.wait_ge(stored[slot].sem, stored[slot].base + uses * 16 * n_stores)

        def node_signals(n_loads, n_stores):
            R = BATCHES // DEPTH
            return ([(loaded[s], 16 * n_loads * (R + (s == 0))) for s in range(DEPTH)]
                    + [(stored[s], 16 * n_stores * (R + (s == 0))) for s in range(DEPTH)])

        LN_SUM, LN_CENTRED, LN_SQUARED, LN_VAR, LN_STD, LN_RSTD = range(6)

        class Norm:

            def __init__(self, k, ctx, pre):
                self.s = ln[k]
                self.sum = sb(f"{pre}_sum", [P, 2, HALF], F32, ctx)
                self.xc = sb(f"{pre}_xc", [P, 2, HALF, F], F32, ctx)
                self.sq = sb(f"{pre}_sq", [P, 2, HALF, F], F32, ctx)
                self.var = sb(f"{pre}_var", [P, 2, HALF], F32, ctx)
                self.std = sb(f"{pre}_std", [P, 2, HALF], F32, ctx)
                self.rstd = sb(f"{pre}_rstd", [P, 2, HALF], F32, ctx)

            def dve_sum(self, dve, n, s, xs):
                dve.tensor_reduce(self.sum[:, s, :], xs, AX.X, ALU.add).then_inc(self.s[LN_SUM].sem, 1)

            def dve_centre(self, dve, n, s, xs):
                dve.wait_ge(self.s[LN_SUM].sem, self.s[LN_SUM].base + n + 1)
                dve.scalar_tensor_tensor(out=self.xc[:, s, :, :], in0=self.sum[:, s, :].unsqueeze(2).to_broadcast([P, HALF, F]),
                                         scalar=-1.0 / F, in1=xs, op0=ALU.mult, op1=ALU.add).then_inc(self.s[LN_CENTRED].sem, 1)

            def act_square(self, act, n, s):
                act.wait_ge(self.s[LN_CENTRED].sem, self.s[LN_CENTRED].base + n + 1)
                if given(n - 1):
                    act.wait_ge(self.s[LN_VAR].sem, self.s[LN_VAR].base + n - 1)
                act.activation(self.sq[:, s, :, :], self.xc[:, s, :, :], ACT.Square, scale=float(F) ** -0.5).then_inc(self.s[LN_SQUARED].sem, 1)

            def dve_var(self, dve, n, s):
                dve.wait_ge(self.s[LN_SQUARED].sem, self.s[LN_SQUARED].base + n + 1)
                dve.tensor_reduce(self.var[:, s, :], self.sq[:, s, :, :], AX.X, ALU.add).then_inc(self.s[LN_VAR].sem, 1)

            def act_std(self, act, n, s):
                act.wait_ge(self.s[LN_VAR].sem, self.s[LN_VAR].base + n + 1)
                if given(n - 1):
                    act.wait_ge(self.s[LN_RSTD].sem, self.s[LN_RSTD].base + n - 1)
                act.activation(self.std[:, s, :], self.var[:, s, :], ACT.Sqrt, bias=eps_t[:, 0:1]).then_inc(self.s[LN_STD].sem, 1)

            def dve_rstd(self, dve, n, s):
                dve.wait_ge(self.s[LN_STD].sem, self.s[LN_STD].base + n + 1)
                dve.reciprocal(self.rstd[:, s, :], self.std[:, s, :]).then_inc(self.s[LN_RSTD].sem, 1)

            def dve_relu(self, dve, n, s, outs, scale=None, ready=None):
                ready = ready or self.s[LN_RSTD]
                dve.wait_ge(ready.sem, ready.base + n + 1)
                scale = self.rstd[:, s, :] if scale is None else scale
                return dve.scalar_tensor_tensor(out=outs, in0=self.xc[:, s, :, :], scalar=0.0,
                                                in1=scale.unsqueeze(2).to_broadcast([P, HALF, F]), op0=ALU.max, op1=ALU.mult)

            def totals(self):
                return [(s, 2 * BATCHES) for s in self.s]

        def gate(engine):
            engine.sem_inc(turn.sem, 1)

        def cols(i, q, s):
            _, b, _ = at(i, q)
            return bass.ds(b * SLOTS + s * HALF, HALF)

        def spread(a):
            return a.unsqueeze(2).to_broadcast([P, HALF, F])

        with ExitStack() as ctx:
            x_in = sb("p0_x", [P, DEPTH, SLOTS * F], F32, ctx)
            h_t = sb("p0_h", [P, DEPTH, SLOTS * F], F32, ctx)
            t_out = sb("p0_t", [P, DEPTH, SLOTS * F], F32, ctx)
            hT = sb("p0_hT", [P, 2, 512], F32, ctx)
            turn_ps = [ps(f"p0_turn{k}", [P, 512], ctx) for k in range(2)]
            lin_ps = [ps(f"p0_lin{k}", [P, 512], ctx) for k in range(2)]
            norm = Norm(0, ctx, "p0")
            block = ctx.enter_context(nc.Block())

            def half(tile, slot, s):
                return halves(tile[:, slot, s * HALF * F:(s + 1) * HALF * F])

            @block.sync
            def _(sp):
                node_streams(sp, [(x, x_in)], [(t0, t_out), (acc0, t_out)], ln[0][LN_CENTRED], t_done)

            @block.vector
            def _(dve):
                def finish(i, q):
                    slot, b, _ = at(i, q)
                    stored_before(dve, i, q, 2)
                    for s in range(2):
                        dve.wait_ge(node_out.sem, node_out.base + 2 * b + s + 1)
                        dve.tensor_tensor(half(t_out, slot, s), halves(lin_ps[s][:, :]), spread(dinv[:, cols(i, q, s)]), ALU.mult).then_inc(t_done.sem, 1)

                def sums_of(i, q):
                    slot, b, uses = at(i, q)
                    dve.wait_ge(loaded[slot].sem, loaded[slot].base + 16 * uses)
                    for s in range(2):
                        if given(2 * b + s - 1):
                            dve.wait_ge(ln[0][LN_CENTRED].sem, ln[0][LN_CENTRED].base + 2 * b + s - 1)
                        norm.dve_sum(dve, 2 * b + s, s, half(x_in, slot, s))

                def body(i, q):
                    slot, b, _ = at(i, q)
                    for s in range(2):
                        if given(2 * b + s - 1):
                            dve.wait_ge(h_new.sem, h_new.base + 2 * b + s - 1)
                        norm.dve_centre(dve, 2 * b + s, s, half(x_in, slot, s))
                    if not isinstance(i, int) or DEPTH * i + q + 1 < BATCHES:
                        sums_of(i + (q + 1) // DEPTH, (q + 1) % DEPTH)
                    for s in range(2):
                        norm.dve_var(dve, 2 * b + s, s)
                    if q or not isinstance(i, int) or i:
                        finish(i + (q - 1) // DEPTH, (q - 1) % DEPTH)
                    for s in range(2):
                        norm.dve_rstd(dve, 2 * b + s, s)
                    if given(2 * (b - DEPTH) + 2):
                        dve.wait_ge(node_turned.sem, node_turned.base + 2 * (b - DEPTH) + 2)
                    for s in range(2):
                        norm.dve_relu(dve, 2 * b + s, s, half(h_t, slot, s)).then_inc(h_new.sem, 1)

                sums_of(0, 0)
                rounds(dve, body, BATCHES)
                finish(BATCHES // DEPTH, 0)

            @block.scalar
            def _(act):
                def body(i, q):
                    _, b, _ = at(i, q)
                    for s in range(2):
                        norm.act_square(act, 2 * b + s, s)
                    for s in range(2):
                        norm.act_std(act, 2 * b + s, s)
                    for s in range(2):
                        act.wait_ge(node_turned.sem, node_turned.base + 2 * b + s + 1)
                        if given(2 * b + s - 1):
                            act.wait_ge(node_out.sem, node_out.base + 2 * b + s - 1)
                        act.activation(hT[:, s, :], turn_ps[s][:, :], ACT.Copy).then_inc(node_copied.sem, 1)

                rounds(act, body, BATCHES)

            @block.tensor
            def _(pe):
                def body(i, q):
                    slot, b, _ = at(i, q)
                    for s in range(2):
                        pe.wait_ge(h_new.sem, h_new.base + 2 * b + s + 1)
                        if given(2 * b + s - 1):
                            pe.wait_ge(node_copied.sem, node_copied.base + 2 * b + s - 1)
                        for k in range(4):
                            at_k = (s * HALF + 2 * k) * F
                            last = pe.transpose(turn_ps[s][:, k * P:(k + 1) * P], h_t[:, slot, at_k:at_k + P], ident[:, :])
                        last.then_inc(node_turned.sem, 1)
                    for s in range(2):
                        pe.wait_ge(node_copied.sem, node_copied.base + 2 * b + s + 1)
                        if given(2 * b + s - 1):
                            pe.wait_ge(t_done.sem, t_done.base + 2 * b + s - 1)
                        pe.matmul(lin_ps[s][:, :], ones3[:, :], b0_parts[:, :], start=True, stop=False, skip_group_check=True)
                        for k in range(4):
                            last = pe.matmul(lin_ps[s][:, k * P:(k + 1) * P], hT[:, s, k * P:(k + 1) * P], w0_pair[:, :],
                                             start=False, stop=k == 3, skip_group_check=True)
                        last.then_inc(node_out.sem, 1)

                rounds(pe, body, BATCHES)

            advance(node_signals(1, 2) + norm.totals()
                    + [(s, 2 * BATCHES) for s in (t_done, h_new, node_turned, node_copied, node_out)])

        def edge_phase(pre, gathers, key, into, into_scale, table, find_into, kind):
            NG = len(gathers)
            AHEAD = 2 if kind == "types" else 1
            LAG = DEPTH if kind else 2

            def uses_of(slot):
                return len(range(slot, GROUPS, DEPTH))

            with ExitStack() as ctx:
                stage = sb(f"{pre}_stage", [P, DEPTH, NG, TILES], I32, ctx)
                keys = sb(f"{pre}_keys", [P, DEPTH, TILES], F32, ctx)
                types = sb(f"{pre}_types", [P, DEPTH, TILES], BF16, ctx) if kind == "types" else None
                into_st = sb(f"{pre}_into", [P, DEPTH, TILES], I32, ctx)
                got = [sb(f"{pre}_got{k}", [P, DEPTH, TILES, F], F32, ctx) for k in range(NG)]
                match = sb(f"{pre}_match", [P, DEPTH, TILES, GROUP], BF16, ctx)
                sums = sb(f"{pre}_sums", [P, DEPTH, TILES * F], F32, ctx)
                diag = sb(f"{pre}_diag", [P, TILES, P], BF16, ctx)
                count_ps = ps(f"{pre}_count", [P, TILES], ctx) if find_into else None
                gap = sb(f"{pre}_gap", [P, TILES], F32, ctx)
                move = sb(f"{pre}_move", [P, TILES], F32, ctx)
                rows_ps = ps(f"{pre}_rows", [P, GROUP], ctx)
                sum_ps = ps(f"{pre}_sum", [P, TILES * F], ctx)
                parts = sb(f"{pre}_parts", [P, DEPTH, 3, TILES * F], BF16, ctx)
                rest = sb(f"{pre}_rest", [P, TILES * F], F32, ctx)
                if kind == "types":
                    type_ps = ps(f"{pre}_type", [P, GROUP], ctx)
                    turn_ps = ps(f"{pre}_turn", [F, GROUP], ctx)
                    msgT_ps = ps(f"{pre}_msgTps", [F, GROUP], ctx)
                    msgT = sb(f"{pre}_msgT", [F, GROUP], F32, ctx)
                    msg = ps(f"{pre}_msgps", [P, TILES * F], ctx)
                    hT = sb(f"{pre}_hT", [P, DEPTH, GROUP], F32, ctx)
                    split = sb(f"{pre}_split", [P, DEPTH, TYPES // 2, GROUP], F32, ctx)
                if kind == "attention":
                    turn_ps = ps(f"{pre}_turn", [F, GROUP], ctx)
                    proj_ps = ps(f"{pre}_proj", [P, TILES, 2 * HEADS * F], ctx)
                    hT = sb(f"{pre}_hT", [F, DEPTH, GROUP], F32, ctx)
                    msg = sb(f"{pre}_msg", [P, TILES * F], F32, ctx)
                    prod = sb(f"{pre}_prod", [P, TILES, HEADS, F], F32, ctx)
                    score = sb(f"{pre}_score", [P, TILES, HEADS], F32, ctx)
                    top = sb(f"{pre}_top", [P, TILES], F32, ctx)
                    below = sb(f"{pre}_below", [P, TILES, HEADS], F32, ctx)
                    ex = sb(f"{pre}_ex", [P, TILES, HEADS], F32, ctx)
                    exs = sb(f"{pre}_exs", [P, TILES], F32, ctx)
                    rex = sb(f"{pre}_rex", [P, TILES], F32, ctx)
                    attn = sb(f"{pre}_attn", [P, TILES, HEADS], F32, ctx)
                freed = {None: [rest_left], "types": [turned], "attention": [turned, att[0]]}[kind]
                block = ctx.enter_context(nc.Block())

                def group_cols(g):
                    return bass.ds(g * TILES, TILES)

                def whole(slot):
                    if kind is None:
                        return got[0][:, slot, :, :].rearrange("p t f -> p (t f)")
                    return msg[:, :]

                def there(i, q, delta):
                    g = at(i, q, delta)[1]
                    return not isinstance(g, int) or g < GROUPS

                @block.scalar
                def _(act):
                    def stage_group(i, q, delta):
                        slot, g, uses = at(i, q, delta)
                        if given((uses - 1) * 16 * TILES * NG):
                            act.wait_ge(gathered[slot].sem, gathered[slot].base + (uses - 1) * 16 * TILES * NG)
                        if given(g - DEPTH + 1):
                            act.wait_ge(matched.sem, matched.base + g - DEPTH + 1)
                        if find_into:
                            if given(g - DEPTH + 1):
                                act.wait_ge(into_known.sem, into_known.base + g - DEPTH + 1)
                        gate(act)
                        for k, (_, rows, scale, offset) in enumerate(gathers):
                            act.activation(stage[:, slot, k, :], rows[:, group_cols(g)], ACT.Copy, scale=scale, bias=offset)
                        if kind == "types":
                            act.activation(types[:, slot, :], type_f[:, group_cols(g)], ACT.Copy)
                        act.activation(keys[:, slot, :], key[:, group_cols(g)], ACT.Copy).then_inc(rows_staged.sem, 1)

                    def copy_turned(i, q, delta):
                        slot, g, _ = at(i, q, delta)
                        act.wait_ge(turned.sem, turned.base + g + 1)
                        used = {"types": by_type, "attention": projected}[kind]
                        if given(g - DEPTH + 1):
                            act.wait_ge(used.sem, used.base + g - DEPTH + 1)
                        if kind == "types":
                            act.activation(hT[F:P, slot, :], turn_ps[:, :], ACT.Copy)
                        act.activation(hT[0:F, slot, :], turn_ps[:, :], ACT.Copy).then_inc(turned_copied.sem, 1)

                    def copy_messages(i, q, delta):
                        _, g, _ = at(i, q, delta)
                        act.wait_ge(messages_turned.sem, messages_turned.base + g + 1)
                        if given(g):
                            act.wait_ge(messages.sem, messages.base + g)
                        act.activation(msgT[:, :], msgT_ps[:, :], ACT.Copy).then_inc(messages_copied.sem, 1)

                    def first_two_parts(i, q, delta):
                        slot, g, uses = at(i, q, delta)
                        if kind is None:
                            act.wait_ge(gathered[slot].sem, gathered[slot].base + uses * 16 * TILES * NG)
                        else:
                            act.wait_ge(messages.sem, messages.base + g + 1)
                        if given(g - DEPTH + 1):
                            act.wait_ge(summed.sem, summed.base + g - DEPTH + 1)
                        gate(act)
                        act.activation(parts[:, slot, 0, :], whole(slot), ACT.Copy).then_inc(first_part.sem, 1)
                        act.wait_ge(rest_left.sem, rest_left.base + g + 1)
                        act.activation(parts[:, slot, 1, :], rest[:, :], ACT.Copy).then_inc(second_part.sem, 1)

                    def body(i, q):
                        slot, g, uses = at(i, q)
                        if there(i, q, AHEAD + 1):
                            stage_group(i, q, AHEAD + 1)
                        if kind == "types":
                            first_two_parts(i, q, 0)
                        if kind == "attention":
                            act.wait_ge(att[2].sem, att[2].base + g + 1)
                            act.activation(ex[:, :, :], below[:, :, :], ACT.Exp).then_inc(att[3].sem, 1)
                        if kind and there(i, q, AHEAD):
                            copy_turned(i, q, AHEAD)
                        if kind is None and there(i, q, 1):
                            first_two_parts(i, q, 1)
                        if kind == "attention":
                            first_two_parts(i, q, 0)
                        if given((uses - 1) * 16 * TILES):
                            act.wait_ge(scattered[slot].sem, scattered[slot].base + (uses - 1) * 16 * TILES)
                        if find_into:
                            act.wait_ge(into_known.sem, into_known.base + g + 1)
                        gate(act)
                        act.activation(into_st[:, slot, :], into[:, group_cols(g)], ACT.Copy, scale=into_scale).then_inc(into_staged.sem, 1)
                        if kind == "types" and there(i, q, 1):
                            copy_messages(i, q, 1)
                        act.wait_ge(summed.sem, summed.base + g + 1)
                        act.activation(sums[:, slot, :], sum_ps[:, :], ACT.Copy).then_inc(sums_copied.sem, 1)

                    stage_group(0, 0, 0)
                    stage_group(0, 0, 1)
                    if kind:
                        copy_turned(0, 0, 0)
                    if kind == "types":
                        stage_group(0, 0, 2)
                        copy_messages(0, 0, 0)
                        copy_turned(0, 0, 1)
                    if kind is None:
                        first_two_parts(0, 0, 0)
                    rounds(act, body, GROUPS, AHEAD + 1)

                @block.gpsimd
                def _(pool):
                    def gather(i, q):
                        slot, g, uses = at(i, q)
                        pool.wait_ge(rows_staged.sem, rows_staged.base + g + 1)
                        for s in freed:
                            if given(g - DEPTH + 1):
                                pool.wait_ge(s.sem, s.base + g - DEPTH + 1)
                        gate(pool)
                        for k, (rows_of, _, _, _) in enumerate(gathers):
                            for t in range(TILES):
                                pool.indirect_dma_start(out=got[k][:, slot, t, :], out_offset=None, in_=rows_of,
                                                        in_offset=bass.IndirectOffsetOnAxis(ap=stage[:, slot, k, t:t + 1].bitcast(U32), axis=0)
                                                        ).then_inc(gathered[slot].sem, 16)

                    def scatter(i, q):
                        slot, g, _ = at(i, q)
                        before, _, uses = at(i, q, -1)
                        pool.wait_ge(sums_copied.sem, sums_copied.base + g + 1)
                        pool.wait_ge(into_staged.sem, into_staged.base + g + 1)
                        if given(uses * 16 * TILES):
                            pool.wait_ge(scattered[before].sem, scattered[before].base + uses * 16 * TILES)
                        gate(pool)
                        for t in range(TILES):
                            pool.indirect_dma_start(out=table, out_offset=bass.IndirectOffsetOnAxis(ap=into_st[:, slot, t:t + 1].bitcast(U32), axis=0),
                                                    in_=sums[:, slot, t * F:(t + 1) * F], in_offset=None,
                                                    compute_op=ALU.add).then_inc(scattered[slot].sem, 16)

                    def body(i, q):
                        gather(i, q)
                        if not isinstance(i, int) or DEPTH * i + q >= LAG:
                            scatter(i + (q - LAG) // DEPTH, (q - LAG) % DEPTH)

                    rounds(pool, body, GROUPS, AHEAD + 1)
                    for g in range(GROUPS - LAG, GROUPS):
                        scatter(g // DEPTH, g % DEPTH)
                    for slot in range(DEPTH):
                        pool.wait_ge(scattered[slot].sem, scattered[slot].base + uses_of(slot) * 16 * TILES)

                @block.tensor
                def _(pe):
                    def spread_keys(i, q, delta):
                        slot, g, _ = at(i, q, delta)
                        pe.wait_ge(rows_staged.sem, rows_staged.base + g + 1)
                        if given(g):
                            pe.wait_ge(matched.sem, matched.base + g)
                        for t in range(TILES):
                            last = pe.transpose(rows_ps[:, t * P:(t + 1) * P], keys[:, slot, t:t + 1].to_broadcast([P, P]), ident[:, :])
                        last.then_inc(keys_spread.sem, 1)

                    def turn_rows(i, q, delta):
                        slot, g, uses = at(i, q, delta)
                        pe.wait_ge(gathered[slot].sem, gathered[slot].base + uses * 16 * TILES * NG)
                        if given(g):
                            pe.wait_ge(turned_copied.sem, turned_copied.base + g)
                        gate(pe)
                        for t in range(TILES):
                            last = pe.transpose(turn_ps[:, t * P:(t + 1) * P], got[0][:, slot, t, :], ident[:, :])
                        last.then_inc(turned.sem, 1)

                    def spread_types(i, q, delta):
                        slot, g, _ = at(i, q, delta)
                        if given(g):
                            pe.wait_ge(by_type.sem, by_type.base + g)
                        for t in range(TILES):
                            last = pe.matmul(type_ps[:, t * P:(t + 1) * P], types[:, slot, t:t + 1].to_broadcast([P, P]), ident_b[:, :],
                                             start=True, stop=True)
                        last.then_inc(types_spread.sem, 1)

                    def type_messages(i, q, delta):
                        slot, g, _ = at(i, q, delta)
                        pe.wait_ge(by_type.sem, by_type.base + g + 1)
                        if given(g):
                            pe.wait_ge(messages_copied.sem, messages_copied.base + g)
                        for c in range(TYPES // 2):
                            last = pe.matmul(msgT_ps[:, :], type_w[:, c, :], split[:, slot, c, :], start=c == 0, stop=c == TYPES // 2 - 1)
                        last.then_inc(messages_turned.sem, 1)

                    def turn_messages(i, q):
                        _, g, _ = at(i, q)
                        pe.wait_ge(messages_copied.sem, messages_copied.base + g + 1)
                        if given(g):
                            pe.wait_ge(rest_left.sem, rest_left.base + g)
                        gate(pe)
                        for t in range(TILES):
                            last = pe.transpose(msg[:, t * F:(t + 1) * F], msgT[:, t * P:(t + 1) * P], ident[0:F, 0:F])
                        last.then_inc(messages.sem, 1)

                    def project(i, q, delta):
                        slot, g, _ = at(i, q, delta)
                        pe.wait_ge(turned_copied.sem, turned_copied.base + g + 1)
                        if given(g):
                            pe.wait_ge(att[6].sem, att[6].base + g)
                        for t in range(TILES):
                            last = pe.matmul(proj_ps[:, t, :], hT[:, slot, t * P:(t + 1) * P], att_w[:, :], start=True, stop=True)
                        last.then_inc(projected.sem, 1)

                    def sum_targets(i, q):
                        slot, g, _ = at(i, q)
                        pe.wait_ge(parts_made.sem, parts_made.base + g + 1)
                        pe.wait_ge(matched.sem, matched.base + g + 1)
                        if given(g):
                            pe.wait_ge(sums_copied.sem, sums_copied.base + g)
                        for b in range(TILES):
                            for a in range(TILES):
                                for k in range(3):
                                    last = pe.matmul(sum_ps[:, b * F:(b + 1) * F], match[:, slot, a, b * P:(b + 1) * P], parts[:, slot, k, a * F:(a + 1) * F],
                                                     start=a == 0 and k == 0, stop=a == TILES - 1 and k == 2)
                        last.then_inc(summed.sem, 1)

                    def count_earlier(i, q, delta):
                        slot, g, _ = at(i, q, delta)
                        pe.wait_ge(diagonal.sem, diagonal.base + g + 1)
                        if given(g):
                            pe.wait_ge(chosen.sem, chosen.base + g)
                        for b in range(TILES):
                            for a in range(b):
                                pe.matmul(count_ps[:, b:b + 1], match[:, slot, a, b * P:(b + 1) * P], ones[:, :], start=a == 0, stop=False)
                            last = pe.matmul(count_ps[:, b:b + 1], diag[:, b, :], ones[:, :], start=b == 0, stop=True)
                        last.then_inc(counted.sem, 1)

                    def prepare(i, q, delta):
                        if kind == "types":
                            spread_types(i, q, delta)
                        if kind:
                            turn_rows(i, q, delta)
                        if kind == "attention":
                            project(i, q, delta)

                    def body(i, q):
                        ahead = there(i, q, AHEAD)
                        if kind == "types":
                            turn_messages(i, q)
                        if ahead:
                            spread_keys(i, q, AHEAD)
                            prepare(i, q, AHEAD)
                        if kind != "types":
                            sum_targets(i, q)
                        elif there(i, q, 1):
                            type_messages(i, q, 1)
                        if ahead and find_into:
                            count_earlier(i, q, AHEAD)
                        if kind == "types":
                            sum_targets(i, q)

                    spread_keys(0, 0, 0)
                    prepare(0, 0, 0)
                    if find_into:
                        count_earlier(0, 0, 0)
                    if kind == "types":
                        type_messages(0, 0, 0)
                        spread_keys(0, 0, 1)
                        prepare(0, 0, 1)
                        count_earlier(0, 0, 1)
                    rounds(pe, body, GROUPS, AHEAD + 1)

                @block.vector
                def _(dve):
                    def match_group(i, q, delta):
                        slot, g, _ = at(i, q, delta)
                        dve.wait_ge(keys_spread.sem, keys_spread.base + g + 1)
                        if given(g - DEPTH + 1):
                            dve.wait_ge(summed.sem, summed.base + g - DEPTH + 1)
                        for a in range(TILES):
                            last = dve.tensor_scalar(match[:, slot, a, :], rows_ps[:, :], keys[:, slot, a:a + 1], None, ALU.is_equal)
                        last.then_inc(matched.sem, 1)
                        if not find_into:
                            return
                        dve.wait_ge(matched.sem, matched.base + g + 1)
                        if given(g):
                            dve.wait_ge(counted.sem, counted.base + g)
                        dve.tensor_tensor(diag[:, :, :], match[:, slot, :, :].rearrange("p a (b c) -> p (a b) c", c=P)[:, 0:TILES * TILES:TILES + 1, :],
                                          earlier[:, :].unsqueeze(1).to_broadcast([P, TILES, P]), ALU.mult).then_inc(diagonal.sem, 1)

                    def choose_rows(i, q, delta):
                        slot, g, _ = at(i, q, delta)
                        if given(g):
                            dve.wait_ge(chosen.sem, chosen.base + g)
                        dve.tensor_tensor(gap[:, :], spare[:, :], keys[:, slot, :], ALU.subtract).then_inc(spared.sem, 1)
                        dve.wait_ge(counted.sem, counted.base + g + 1)
                        dve.wait_ge(spared.sem, spared.base + g + 1)
                        dve.scalar_tensor_tensor(out=move[:, :], in0=count_ps[:, :], scalar=0.5, in1=gap[:, :], op0=ALU.is_gt, op1=ALU.mult).then_inc(chosen.sem, 1)
                        dve.wait_ge(chosen.sem, chosen.base + g + 1)
                        dve.tensor_tensor(into[:, group_cols(g)], move[:, :], keys[:, slot, :], ALU.add).then_inc(into_known.sem, 1)

                    def split_types(i, q, delta):
                        slot, g, _ = at(i, q, delta)
                        dve.wait_ge(types_spread.sem, types_spread.base + g + 1)
                        dve.wait_ge(turned_copied.sem, turned_copied.base + g + 1)
                        if given(g - DEPTH + 1):
                            dve.wait_ge(messages_turned.sem, messages_turned.base + g - DEPTH + 1)
                        for c in range(TYPES // 2):
                            last = dve.scalar_tensor_tensor(out=split[:, slot, c, :], in0=type_ps[:, :], scalar=type_of[:, c:c + 1], in1=hT[:, slot, :],
                                                            op0=ALU.is_equal, op1=ALU.mult)
                        last.then_inc(by_type.sem, 1)

                    def attend(i, q):
                        slot, g, uses = at(i, q)
                        dve.wait_ge(projected.sem, projected.base + g + 1)
                        dve.wait_ge(gathered[slot].sem, gathered[slot].base + uses * 16 * TILES * NG)
                        if given(g):
                            dve.wait_ge(messages.sem, messages.base + g)
                        by_head = proj_ps[:, :, 0:HEADS * F].rearrange("p t (h f) -> p t h f", h=HEADS)
                        for t in range(TILES):
                            last = dve.tensor_tensor(prod[:, t, :, :], by_head[:, t, :, :], got[1][:, slot, t, :].unsqueeze(1).to_broadcast([P, HEADS, F]), ALU.mult)
                        last.then_inc(att[0].sem, 1)
                        dve.wait_ge(att[0].sem, att[0].base + g + 1)
                        dve.tensor_reduce(score[:, :, :], prod[:, :, :, :], AX.X, ALU.add).then_inc(att[1].sem, 1)
                        dve.wait_ge(att[1].sem, att[1].base + g + 1)
                        dve.tensor_reduce(top[:, :], score[:, :, :], AX.X, ALU.max).then_inc(att[4].sem, 1)
                        dve.wait_ge(att[4].sem, att[4].base + 3 * g + 1)
                        dve.tensor_tensor(below[:, :, :], score[:, :, :], top[:, :].unsqueeze(2).to_broadcast([P, TILES, HEADS]), ALU.subtract).then_inc(att[2].sem, 1)
                        dve.wait_ge(att[3].sem, att[3].base + g + 1)
                        dve.tensor_reduce(exs[:, :], ex[:, :, :], AX.X, ALU.add).then_inc(att[4].sem, 1)
                        dve.wait_ge(att[4].sem, att[4].base + 3 * g + 2)
                        dve.reciprocal(rex[:, :], exs[:, :]).then_inc(att[4].sem, 1)
                        if given(3 * g + 3):
                            dve.wait_ge(att[4].sem, att[4].base + 3 * g + 3)
                        dve.tensor_tensor(attn[:, :, :], ex[:, :, :], rex[:, :].unsqueeze(2).to_broadcast([P, TILES, HEADS]), ALU.mult).then_inc(att[5].sem, 1)
                        dve.wait_ge(att[5].sem, att[5].base + g + 1)
                        values = proj_ps[:, :, HEADS * F:2 * HEADS * F].rearrange("p t (h f) -> p t h f", h=HEADS)
                        for t in range(TILES):
                            last = dve.tensor_tensor(prod[:, t, :, :], values[:, t, :, :], attn[:, t, :].unsqueeze(2).to_broadcast([P, HEADS, F]), ALU.mult)
                        last.then_inc(att[6].sem, 1)
                        dve.wait_ge(att[6].sem, att[6].base + g + 1)
                        if given(g):
                            dve.wait_ge(rest_left.sem, rest_left.base + g)
                        dve.tensor_reduce(msg[:, :].rearrange("p (t f) -> p t f", f=F), prod[:, :, :, :].rearrange("p t h f -> p t f h"), AX.X, ALU.add).then_inc(messages.sem, 1)

                    def leave_rest(i, q, delta):
                        slot, g, _ = at(i, q, delta)
                        dve.wait_ge(first_part.sem, first_part.base + g + 1)
                        if given(g):
                            dve.wait_ge(parts_made.sem, parts_made.base + g)
                        dve.tensor_tensor(rest[:, :], whole(slot), parts[:, slot, 0, :], ALU.subtract).then_inc(rest_left.sem, 1)

                    def third_part(i, q, delta):
                        slot, g, _ = at(i, q, delta)
                        dve.wait_ge(second_part.sem, second_part.base + g + 1)
                        dve.tensor_tensor(parts[:, slot, 2, :], rest[:, :], parts[:, slot, 1, :], ALU.subtract).then_inc(parts_made.sem, 1)

                    def body(i, q):
                        ahead = there(i, q, AHEAD)
                        if find_into and there(i, q, AHEAD - 1):
                            choose_rows(i, q, AHEAD - 1)
                        if kind is None:
                            if ahead:
                                leave_rest(i, q, 1)
                                match_group(i, q, 1)
                                third_part(i, q, 1)
                            return
                        if kind == "attention":
                            attend(i, q)
                        else:
                            leave_rest(i, q, 0)
                        if ahead:
                            match_group(i, q, AHEAD)
                        if kind == "attention":
                            leave_rest(i, q, 0)
                        third_part(i, q, 0)
                        if kind == "types" and ahead:
                            split_types(i, q, AHEAD)

                    match_group(0, 0, 0)
                    if kind is None:
                        leave_rest(0, 0, 0)
                        third_part(0, 0, 0)
                    if kind == "types":
                        split_types(0, 0, 0)
                        choose_rows(0, 0, 0)
                        match_group(0, 0, 1)
                        split_types(0, 0, 1)
                    rounds(dve, body, GROUPS, AHEAD + 1)

            totals = [(gathered[k], uses_of(k) * 16 * TILES * NG) for k in range(DEPTH)]
            totals += [(scattered[k], uses_of(k) * 16 * TILES) for k in range(DEPTH)]
            totals += [(s, GROUPS) for s in (rows_staged, keys_spread, matched, into_staged, summed, sums_copied,
                                             first_part, rest_left, second_part, parts_made)]
            if find_into:
                totals += [(s, GROUPS) for s in (diagonal, counted, spared, chosen, into_known)]
            if kind:
                totals += [(s, GROUPS) for s in (turned, turned_copied, messages)]
            if kind == "types":
                totals += [(s, GROUPS) for s in (types_spread, by_type, messages_turned, messages_copied)]
            if kind == "attention":
                totals += [(s, GROUPS) for s in (projected, att[0], att[1], att[2], att[3], att[5], att[6])] + [(att[4], 3 * GROUPS)]
            advance(totals)

        edge_phase("e0", [(t0, dst_row, 1.0, 0.0)], src_key, src_into, 1.0, acc0, True, None)

        with ExitStack() as ctx:
            x_in = sb("p1_x", [P, DEPTH, SLOTS * F], F32, ctx)
            a_in = sb("p1_a", [P, DEPTH, SLOTS * F], F32, ctx)
            x_out = sb("p1_xo", [P, DEPTH, SLOTS * F], F32, ctx)
            mh_out = sb("p1_mh", [P, DEPTH, SLOTS * 2 * F], F32, ctx)
            scaled = sb("p1_sc", [P, 2, HALF, F], F32, ctx)
            norm = Norm(0, ctx, "p1")
            block = ctx.enter_context(nc.Block())

            @block.sync
            def _(sp):
                node_streams(sp, [(x, x_in), (acc0, a_in)], [(x1, x_out), (mh1, mh_out)], x_new, h_new)

            @block.gpsimd
            def _(pool):
                def body(i, q):
                    slot, b, uses = at(i, q)
                    for s in range(2):
                        pool.wait_ge(loaded[slot].sem, loaded[slot].base + 2 * 16 * uses)
                        if given(2 * b + s - 1):
                            pool.wait_ge(x_new.sem, x_new.base + 2 * b + s - 1)
                        gate(pool)
                        pool.tensor_tensor(scaled[:, s, :, :], half(a_in, slot, s), spread(dinv[:, cols(i, q, s)]), ALU.mult).then_inc(mixed.sem, 1)

                rounds(pool, body, BATCHES)

            @block.vector
            def _(dve):
                def new_x(i, q):
                    slot, b, _ = at(i, q)
                    stored_before(dve, i, q, 2)
                    for s in range(2):
                        dve.wait_ge(mixed.sem, mixed.base + 2 * b + s + 1)
                        dve.tensor_tensor(half(x_out, slot, s), half(x_in, slot, s), scaled[:, s, :, :], ALU.add).then_inc(x_new.sem, 1)

                def moments(i, q):
                    slot, b, _ = at(i, q)
                    for s in range(2):
                        dve.wait_ge(x_new.sem, x_new.base + 2 * b + s + 1)
                        norm.dve_sum(dve, 2 * b + s, s, half(x_out, slot, s))
                    for s in range(2):
                        norm.dve_centre(dve, 2 * b + s, s, half(x_out, slot, s))
                    for s in range(2):
                        norm.dve_var(dve, 2 * b + s, s)

                def new_h(i, q):
                    slot, b, _ = at(i, q)
                    for s in range(2):
                        norm.dve_rstd(dve, 2 * b + s, s)
                    for s in range(2):
                        o = halves(mh_out[:, slot, s * HALF * 2 * F:(s + 1) * HALF * 2 * F], 2 * F)[:, :, F:2 * F]
                        norm.dve_relu(dve, 2 * b + s, s, o).then_inc(h_new.sem, 1)

                def body(i, q):
                    first = isinstance(i, int) and i == 0 and q == 0
                    before = (i + (q - 1) // DEPTH, (q - 1) % DEPTH)
                    if not first:
                        moments(*before)
                    new_x(i, q)
                    if not first:
                        new_h(*before)

                dve.memset(mh_out[:, :, :], 0.0).then_inc(step[0].sem, 1)
                dve.wait_ge(step[0].sem, step[0].base + 1)
                rounds(dve, body, BATCHES)
                moments(BATCHES // DEPTH, 0)
                new_h(BATCHES // DEPTH, 0)

            @block.scalar
            def _(act):
                def body(i, q):
                    _, b, _ = at(i, q)
                    for s in range(2):
                        norm.act_square(act, 2 * b + s, s)
                    for s in range(2):
                        norm.act_std(act, 2 * b + s, s)

                rounds(act, body, BATCHES)

            advance(node_signals(2, 2) + norm.totals() + [(s, 2 * BATCHES) for s in (mixed, x_new, h_new)] + [(step[0], 1)])

        edge_phase("e1", [(mh1_rows, src_row, 2.0, 1.0)], dst_key, dst_into, 2.0, mh1_rows, True, "types")

        QUAD = 4
        with ExitStack() as ctx:
            x_in = sb("p2_x", [P, DEPTH, SLOTS * F], F32, ctx)
            mh_in = sb("p2_mh", [P, DEPTH, SLOTS * 2 * F], F32, ctx)
            x_out = sb("p2_xo", [P, DEPTH, SLOTS * F], F32, ctx)
            h_out = sb("p2_ho", [P, DEPTH, SLOTS * F], F32, ctx)
            mhT = sb("p2_mhT", [P, 2, QUAD * P], F32, ctx)
            rz = sb("p2_rz", [P, DEPTH, SLOTS, 2 * F], F32, ctx)
            cand = sb("p2_cand", [P, DEPTH, SLOTS, F], F32, ctx)
            blend = sb("p2_blend", [P, DEPTH, SLOTS, F], F32, ctx)
            turn_ps = [ps(f"p2_turn{k}", [P, QUAD * P], ctx) for k in range(2)]
            gate_ps = [ps(f"p2_gate{k}", [P, QUAD, 4 * F], ctx) for k in range(2)]
            norm = Norm(0, ctx, "p2")
            rz_done, reset_done, cand_in, cand_done, diff_done, blended = step
            keep = mixed
            block = ctx.enter_context(nc.Block())

            def there(i, q, delta):
                b = at(i, q, delta)[1]
                return not isinstance(b, int) or 0 <= b < BATCHES

            def mh_half(slot, s):
                return halves(mh_in[:, slot, s * HALF * 2 * F:(s + 1) * HALF * 2 * F], 2 * F)

            @block.sync
            def _(sp):
                node_streams(sp, [(x1, x_in), (mh1, mh_in)], [(x2, x_out), (h2, h_out), (acc2, h_out)], x_new, h_new, DEPTH)

            @block.tensor
            def _(pe):
                def turn_quad(i, q, delta, t):
                    slot, b, uses = at(i, q, delta)
                    m = 4 * b + t
                    pe.wait_ge(loaded[slot].sem, loaded[slot].base + 2 * 16 * uses)
                    if given(m - 1):
                        pe.wait_ge(node_copied.sem, node_copied.base + m - 1)
                    for k in range(QUAD):
                        c = (t * QUAD + k) * P
                        last = pe.transpose(turn_ps[t % 2][:, k * P:(k + 1) * P], mh_in[:, slot, c:c + P], ident[:, :])
                    last.then_inc(node_turned.sem, 1)

                def body(i, q):
                    _, b, _ = at(i, q)
                    for t in range(4):
                        m = 4 * b + t
                        if t < 3:
                            turn_quad(i, q, 0, t + 1)
                        elif there(i, q, 1):
                            turn_quad(i, q, 1, 0)
                        pe.wait_ge(node_copied.sem, node_copied.base + m + 1)
                        if given(m - 1):
                            pe.wait_ge(rz_done.sem, rz_done.base + m - 1)
                        if given(m - 1):
                            pe.wait_ge(cand_in.sem, cand_in.base + m - 1)
                        for j in range(2):
                            two = gate_ps[t % 2][:, 2 * j:2 * j + 2, :].rearrange("p k f -> p (k f)")
                            pe.matmul(two, ones3[:, :], gate_b_parts[:, :], start=True, stop=False, skip_group_check=True)
                            for k in (2 * j, 2 * j + 1):
                                last = pe.matmul(gate_ps[t % 2][:, k, :], mhT[:, t % 2, k * P:(k + 1) * P], gate_w[:, :],
                                                 start=False, stop=k % 2 == 1, skip_group_check=True)
                        last.then_inc(node_out.sem, 1)

                turn_quad(0, 0, 0, 0)
                rounds(pe, body, BATCHES)

            @block.scalar
            def _(act):
                def copy_quad(i, q, delta, t):
                    m = 4 * at(i, q, delta)[1] + t
                    act.wait_ge(node_turned.sem, node_turned.base + m + 1)
                    if given(m - 1):
                        act.wait_ge(node_out.sem, node_out.base + m - 1)
                    act.activation(mhT[:, t % 2, :], turn_ps[t % 2][:, :], ACT.Copy).then_inc(node_copied.sem, 1)

                def sigmoid_quad(i, q, t):
                    slot, b, _ = at(i, q)
                    act.wait_ge(node_out.sem, node_out.base + 4 * b + t + 1)
                    if t == 0:
                        if given(2 * (b - DEPTH) + 2):
                            act.wait_ge(blended.sem, blended.base + 2 * (b - DEPTH) + 2)
                    act.activation(rz[:, slot, t * QUAD:(t + 1) * QUAD, :], gate_ps[t % 2][:, :, 0:2 * F], ACT.Sigmoid).then_inc(rz_done.sem, 1)

                def tanh_half(i, q, delta, s):
                    slot, b, _ = at(i, q, delta)
                    act.wait_ge(cand_in.sem, cand_in.base + 4 * b + 2 * s + 2)
                    a = cand[:, slot, s * HALF:(s + 1) * HALF, :]
                    act.activation(a, a, ACT.Tanh).then_inc(cand_done.sem, 1)

                def body(i, q):
                    now, one, two = there(i, q, 0), there(i, q, -1), there(i, q, -2)
                    if now:
                        copy_quad(i, q, 0, 1)
                    if one:
                        tanh_half(i, q, -1, 1)
                    if now:
                        sigmoid_quad(i, q, 0)
                        copy_quad(i, q, 0, 2)
                    if two:
                        for s in range(2):
                            norm.act_square(act, 2 * at(i, q, -2)[1] + s, s)
                    if now:
                        sigmoid_quad(i, q, 1)
                        copy_quad(i, q, 0, 3)
                        sigmoid_quad(i, q, 2)
                        tanh_half(i, q, 0, 0)
                    if there(i, q, 1):
                        copy_quad(i, q, 1, 0)
                    if two:
                        for s in range(2):
                            norm.act_std(act, 2 * at(i, q, -2)[1] + s, s)
                    if now:
                        sigmoid_quad(i, q, 3)

                copy_quad(0, 0, 0, 0)
                rounds(act, body, BATCHES)
                body(BATCHES // DEPTH, 1)
                body(BATCHES // DEPTH, 2)

            @block.gpsimd
            def _(pool):
                def body(i, q):
                    slot, b, uses = at(i, q)
                    for s in range(2):
                        n = 2 * b + s
                        z = rz[:, slot, s * HALF:(s + 1) * HALF, F:2 * F]
                        c = cand[:, slot, s * HALF:(s + 1) * HALF, :]
                        o = blend[:, slot, s * HALF:(s + 1) * HALF, :]
                        pool.wait_ge(cand_done.sem, cand_done.base + n + 1)
                        if given(n - 2 * DEPTH + 1):
                            pool.wait_ge(x_new.sem, x_new.base + n - 2 * DEPTH + 1)
                        pool.tensor_tensor(o, mh_half(slot, s)[:, :, F:2 * F], c, ALU.subtract).then_inc(diff_done.sem, 1)
                        pool.wait_ge(diff_done.sem, diff_done.base + n + 1)
                        pool.tensor_tensor(o, o, z, ALU.mult).then_inc(blended.sem, 1)
                        pool.tensor_tensor(half(x_in, slot, s), half(x_in, slot, s), c, ALU.add).then_inc(keep.sem, 1)

                rounds(pool, body, BATCHES)

            @block.vector
            def _(dve):
                def gates(i, q, t):
                    slot, b, _ = at(i, q)
                    m = 4 * b + t
                    a = cand[:, slot, t * QUAD:(t + 1) * QUAD, :]
                    dve.wait_ge(rz_done.sem, rz_done.base + m + 1)
                    if t == 0:
                        if given(2 * (b - DEPTH) + 2):
                            dve.wait_ge(keep.sem, keep.base + 2 * (b - DEPTH) + 2)
                    dve.tensor_tensor(a, gate_ps[t % 2][:, :, 3 * F:4 * F], rz[:, slot, t * QUAD:(t + 1) * QUAD, 0:F], ALU.mult).then_inc(reset_done.sem, 1)
                    dve.wait_ge(reset_done.sem, reset_done.base + m + 1)
                    dve.tensor_tensor(a, gate_ps[t % 2][:, :, 2 * F:3 * F], a, ALU.add).then_inc(cand_in.sem, 1)

                def new_x(i, q, delta, s):
                    slot, b, _ = at(i, q, delta)
                    if s == 0:
                        stored_before(dve, i + (q + delta) // DEPTH, (q + delta) % DEPTH, 3)
                    dve.wait_ge(keep.sem, keep.base + 2 * b + s + 1)
                    dve.tensor_tensor(half(x_out, slot, s), blend[:, slot, s * HALF:(s + 1) * HALF, :], half(x_in, slot, s), ALU.add).then_inc(x_new.sem, 1)

                def body(i, q):
                    now, one, two = there(i, q, 0), there(i, q, -1), there(i, q, -2)
                    slot_1, b_1, _ = at(i, q, -1)
                    slot_2, b_2, _ = at(i, q, -2)
                    if now:
                        gates(i, q, 0)
                    if one:
                        new_x(i, q, -1, 0)
                    if now:
                        gates(i, q, 1)
                    if two:
                        for s in range(2):
                            norm.dve_var(dve, 2 * b_2 + s, s)
                    if one:
                        new_x(i, q, -1, 1)
                    if now:
                        gates(i, q, 2)
                    if one:
                        for s in range(2):
                            dve.wait_ge(x_new.sem, x_new.base + 2 * b_1 + s + 1)
                            norm.dve_sum(dve, 2 * b_1 + s, s, half(x_out, slot_1, s))
                    if now:
                        gates(i, q, 3)
                    if two:
                        for s in range(2):
                            norm.dve_rstd(dve, 2 * b_2 + s, s)
                        for s in range(2):
                            norm.dve_relu(dve, 2 * b_2 + s, s, half(h_out, slot_2, s)).then_inc(h_new.sem, 1)
                    if one:
                        for s in range(2):
                            if given(2 * b_2 + s + 1):
                                dve.wait_ge(h_new.sem, h_new.base + 2 * b_2 + s + 1)
                            norm.dve_centre(dve, 2 * b_1 + s, s, half(x_out, slot_1, s))

                rounds(dve, body, BATCHES)
                body(BATCHES // DEPTH, 1)
                body(BATCHES // DEPTH, 2)

            advance(node_signals(2, 3) + norm.totals()
                    + [(s, 4 * BATCHES) for s in (node_turned, node_copied, node_out, rz_done, reset_done, cand_in)]
                    + [(s, 2 * BATCHES) for s in (cand_done, diff_done, blended, keep, x_new, h_new)])

        edge_phase("e2", [(h2, src_row, 1.0, 0.0), (h2, dst_row, 1.0, 0.0)], dst_key, dst_into, 1.0, acc2, False, "attention")

        with ExitStack() as ctx:
            x_in = sb("p3_x", [P, DEPTH, SLOTS * F], F32, ctx)
            a_in = sb("p3_a", [P, DEPTH, SLOTS * F], F32, ctx)
            x_out = sb("p3_xo", [P, DEPTH, SLOTS * F], F32, ctx)
            u_out = sb("p3_u", [P, DEPTH, SLOTS * F], F32, ctx)
            y = sb("p3_y", [P, 2, HALF, F], F32, ctx)
            scale = sb("p3_scale", [P, 2, HALF], F32, ctx)
            norm_a, norm_x = Norm(0, ctx, "p3a"), Norm(1, ctx, "p3x")
            x_beta, normed, gamma_done, scale_done = step[0], step[1], step[2], step[3]
            block = ctx.enter_context(nc.Block())

            def row_of(k):
                return gb_rows[:, k, :].unsqueeze(1).to_broadcast([P, HALF, F])

            @block.sync
            def _(sp):
                node_streams(sp, [(x2, x_in), (acc2, a_in)], [(x3, x_out), (u3, u_out)], x_new, h_new)

            @block.scalar
            def _(act):
                def body(i, q):
                    _, b, _ = at(i, q)
                    if not isinstance(b, int) or b < BATCHES:
                        for s in range(2):
                            norm_a.act_square(act, 2 * b + s, s)
                        for s in range(2):
                            norm_a.act_std(act, 2 * b + s, s)
                    if not isinstance(b, int) or b > 0:
                        for s in range(2):
                            norm_x.act_square(act, 2 * (b - 1) + s, s)
                        for s in range(2):
                            norm_x.act_std(act, 2 * (b - 1) + s, s)

                rounds(act, body, BATCHES)
                body(BATCHES // DEPTH, 1)

            @block.gpsimd
            def _(pool):
                def body(i, q):
                    slot, b, uses = at(i, q)
                    pool.wait_ge(loaded[slot].sem, loaded[slot].base + 2 * 16 * uses)
                    for s in range(2):
                        pool.tensor_tensor(half(x_in, slot, s), half(x_in, slot, s), row_of(1), ALU.add).then_inc(x_beta.sem, 1)
                    for s in range(2):
                        n = 2 * b + s
                        pool.wait_ge(norm_a.s[LN_RSTD].sem, norm_a.s[LN_RSTD].base + n + 1)
                        if given(n - 1):
                            pool.wait_ge(x_new.sem, x_new.base + n - 1)
                        pool.tensor_tensor(y[:, s, :, :], norm_a.xc[:, s, :, :], spread(norm_a.rstd[:, s, :]), ALU.mult).then_inc(normed.sem, 1)
                        pool.wait_ge(normed.sem, normed.base + n + 1)
                        pool.tensor_tensor(y[:, s, :, :], y[:, s, :, :], row_of(0), ALU.mult).then_inc(gamma_done.sem, 1)

                rounds(pool, body, BATCHES)

            @block.vector
            def _(dve):
                def second(i, q, part):
                    slot, b, _ = at(i, q)
                    for s in range(2):
                        n = 2 * b + s
                        if part == 0:
                            if s == 0:
                                stored_before(dve, i, q, 2)
                            dve.wait_ge(gamma_done.sem, gamma_done.base + n + 1)
                            dve.wait_ge(x_beta.sem, x_beta.base + n + 1)
                            dve.tensor_tensor(half(x_out, slot, s), half(x_in, slot, s), y[:, s, :, :], ALU.add).then_inc(x_new.sem, 1)
                        elif part == 1:
                            dve.wait_ge(x_new.sem, x_new.base + n + 1)
                            norm_x.dve_sum(dve, n, s, half(x_out, slot, s))
                        elif part == 2:
                            norm_x.dve_centre(dve, n, s, half(x_out, slot, s))
                        elif part == 3:
                            norm_x.dve_var(dve, n, s)
                        elif part == 4:
                            norm_x.dve_rstd(dve, n, s)
                        elif part == 5:
                            dve.wait_ge(norm_x.s[LN_RSTD].sem, norm_x.s[LN_RSTD].base + n + 1)
                            dve.tensor_tensor(scale[:, s, :], norm_x.rstd[:, s, :], inv_s[:, cols(i, q, s)], ALU.mult).then_inc(scale_done.sem, 1)
                        else:
                            norm_x.dve_relu(dve, n, s, half(u_out, slot, s), scale[:, s, :], scale_done).then_inc(h_new.sem, 1)

                def first(i, q, part):
                    slot, b, uses = at(i, q)
                    for s in range(2):
                        n = 2 * b + s
                        if part == 0:
                            dve.wait_ge(loaded[slot].sem, loaded[slot].base + 2 * 16 * uses)
                            norm_a.dve_sum(dve, n, s, half(a_in, slot, s))
                        elif part == 1:
                            if given(n - 1):
                                dve.wait_ge(normed.sem, normed.base + n - 1)
                            norm_a.dve_centre(dve, n, s, half(a_in, slot, s))
                        elif part == 2:
                            norm_a.dve_var(dve, n, s)
                        else:
                            norm_a.dve_rstd(dve, n, s)

                def body(i, q):
                    begun = not (isinstance(i, int) and i == 0 and q == 0)
                    before = (i + (q - 1) // DEPTH, (q - 1) % DEPTH)
                    first(i, q, 1)
                    if begun:
                        second(*before, 0)
                        second(*before, 1)
                    first(i, q, 2)
                    if begun:
                        second(*before, 2)
                    first(i, q, 3)
                    if not isinstance(i, int) or DEPTH * i + q + 1 < BATCHES:
                        first(i + (q + 1) // DEPTH, (q + 1) % DEPTH, 0)
                    if begun:
                        for part in (3, 4, 5, 6):
                            second(*before, part)

                first(0, 0, 0)
                rounds(dve, body, BATCHES)
                for part in range(7):
                    second(BATCHES // DEPTH, 0, part)

            advance(node_signals(2, 2) + norm_a.totals() + norm_x.totals()
                    + [(s, 2 * BATCHES) for s in (x_beta, normed, gamma_done, scale_done, x_new, h_new)])

        edge_phase("e3", [(u3, src_row, 1.0, 0.0)], dst_key, dst_into, 1.0, acc3, False, None)

        with ExitStack() as ctx:
            x_in = sb("p4_x", [P, DEPTH, SLOTS * F], F32, ctx)
            u_in = sb("p4_u", [P, DEPTH, SLOTS * F], F32, ctx)
            a_in = sb("p4_a", [P, DEPTH, SLOTS * F], F32, ctx)
            x_out = sb("p4_xo", [P, DEPTH, SLOTS * F], F32, ctx)
            both = sb("p4_both", [P, 2, HALF, 2 * F], F32, ctx)
            own_h = sb("p4_h", [P, 2, HALF, F], F32, ctx)
            own_a = sb("p4_ha", [P, 2, HALF, F], F32, ctx)
            bothT = sb("p4_bT", [P, 2, HALF * P], F32, ctx)
            leaky = sb("p4_leaky", [P, 2, HALF * F], F32, ctx)
            turn_ps = [ps(f"p4_turn{k}", [P, HALF * P], ctx) for k in range(2)]
            lin_ps = [ps(f"p4_lin{k}", [P, HALF * F], ctx) for k in range(2)]
            acc_scaled, h_scaled, left, right, bent, lin_copied = step
            block = ctx.enter_context(nc.Block())

            @block.sync
            def _(sp):
                node_streams(sp, [(x3, x_in), (u3, u_in), (acc3, a_in)], [(out, x_out)], x_new, x_new)

            @block.gpsimd
            def _(pool):
                def body(i, q):
                    slot, b, uses = at(i, q)
                    for s in range(2):
                        n = 2 * b + s
                        pool.wait_ge(loaded[slot].sem, loaded[slot].base + 3 * 16 * uses)
                        if given(n - 1):
                            pool.wait_ge(left.sem, left.base + n - 1)
                        if given(n - 1):
                            pool.wait_ge(node_turned.sem, node_turned.base + n - 1)
                        gate(pool)
                        pool.tensor_tensor(own_a[:, s, :, :], half(a_in, slot, s), spread(inv_s[:, cols(i, q, s)]), ALU.mult).then_inc(acc_scaled.sem, 1)
                        pool.tensor_tensor(both[:, s, :, F:2 * F], half(a_in, slot, s), half(u_in, slot, s), ALU.mult).then_inc(right.sem, 1)

                rounds(pool, body, BATCHES)

            @block.vector
            def _(dve):
                def finish(i, q):
                    slot, b, _ = at(i, q)
                    stored_before(dve, i, q, 1)
                    for s in range(2):
                        dve.wait_ge(lin_copied.sem, lin_copied.base + 2 * b + s + 1)
                        dve.scalar_tensor_tensor(out=leaky[:, s, :], in0=leaky[:, s, :], scalar=LEAKY, in1=leaky[:, s, :],
                                                 op0=ALU.mult, op1=ALU.max).then_inc(bent.sem, 1)
                    for s in range(2):
                        dve.wait_ge(bent.sem, bent.base + 2 * b + s + 1)
                        dve.tensor_tensor(half(x_out, slot, s), half(x_in, slot, s), halves(leaky[:, s, :]), ALU.add).then_inc(x_new.sem, 1)

                def body(i, q):
                    slot, b, uses = at(i, q)
                    dve.wait_ge(loaded[slot].sem, loaded[slot].base + 3 * 16 * uses)
                    for s in range(2):
                        if given(2 * b + s - 1):
                            dve.wait_ge(left.sem, left.base + 2 * b + s - 1)
                        dve.tensor_tensor(own_h[:, s, :, :], half(u_in, slot, s), spread(sqrt_s[:, cols(i, q, s)]), ALU.mult).then_inc(h_scaled.sem, 1)
                    for s in range(2):
                        n = 2 * b + s
                        dve.wait_ge(h_scaled.sem, h_scaled.base + n + 1)
                        dve.wait_ge(acc_scaled.sem, acc_scaled.base + n + 1)
                        if given(n - 1):
                            dve.wait_ge(node_turned.sem, node_turned.base + n - 1)
                        dve.tensor_tensor(both[:, s, :, 0:F], own_h[:, s, :, :], own_a[:, s, :, :], ALU.add).then_inc(left.sem, 1)
                    if not (isinstance(i, int) and i == 0 and q == 0):
                        finish(i + (q - 1) // DEPTH, (q - 1) % DEPTH)

                rounds(dve, body, BATCHES)
                finish(BATCHES // DEPTH, 0)

            @block.tensor
            def _(pe):
                def body(i, q):
                    _, b, _ = at(i, q)
                    for s in range(2):
                        n = 2 * b + s
                        pe.wait_ge(left.sem, left.base + n + 1)
                        pe.wait_ge(right.sem, right.base + n + 1)
                        if given(n - 1):
                            pe.wait_ge(node_copied.sem, node_copied.base + n - 1)
                        for k in range(HALF):
                            last = pe.transpose(turn_ps[s][:, k * P:(k + 1) * P], both[:, s, k, :], ident[:, :])
                        last.then_inc(node_turned.sem, 1)
                    for s in range(2):
                        n = 2 * b + s
                        pe.wait_ge(node_copied.sem, node_copied.base + n + 1)
                        if given(n - 1):
                            pe.wait_ge(lin_copied.sem, lin_copied.base + n - 1)
                        for k in range(HALF):
                            last = pe.matmul(lin_ps[s][:, k * F:(k + 1) * F], bothT[:, s, k * P:(k + 1) * P], w12[:, :], start=True, stop=True)
                        last.then_inc(node_out.sem, 1)

                rounds(pe, body, BATCHES)

            @block.scalar
            def _(act):
                def body(i, q):
                    _, b, _ = at(i, q)
                    for s in range(2):
                        n = 2 * b + s
                        act.wait_ge(node_turned.sem, node_turned.base + n + 1)
                        if given(n - 1):
                            act.wait_ge(node_out.sem, node_out.base + n - 1)
                        act.activation(bothT[:, s, :], turn_ps[s][:, :], ACT.Copy).then_inc(node_copied.sem, 1)
                    for s in range(2):
                        n = 2 * b + s
                        act.wait_ge(node_out.sem, node_out.base + n + 1)
                        if given(n - 1):
                            act.wait_ge(x_new.sem, x_new.base + n - 1)
                        act.activation(leaky[:, s, :], lin_ps[s][:, :], ACT.Copy).then_inc(lin_copied.sem, 1)

                rounds(act, body, BATCHES)


def kernel(x, src, dst, edge_type_8, L0_gnn_W, L0_gnn_b, L1_gnn_edge_matrix, L1_gnn_w_ih, L1_gnn_w_hh,
           L1_gnn_b_ih, L1_gnn_b_hh, L2_gnn_Wq, L2_gnn_Wk, L2_gnn_Wv, L2_gnn_Wo, L2_gnn_gamma,
           L2_gnn_beta, L3_gnn_W1, L3_gnn_W2):
    import numpy as np
    import concourse.bacc as bacc
    from concourse.bass_utils import run_bass_kernel_spmd

    by_type = np.asarray(L1_gnn_edge_matrix).reshape(TYPES, F, F).transpose(0, 2, 1).reshape(TYPES * F, F)
    arrays = {
        "x": x, "src": src, "dst": dst, "edge_type": edge_type_8,
        "w0t": np.asarray(L0_gnn_W).T, "b0": L0_gnn_b, "at_w": by_type,
        "w_iht": np.asarray(L1_gnn_w_ih).T, "w_hht": np.asarray(L1_gnn_w_hh).T,
        "b_ih": L1_gnn_b_ih, "b_hh": L1_gnn_b_hh,
        "wqt": np.asarray(L2_gnn_Wq).T, "wkt": np.asarray(L2_gnn_Wk).T, "wvt": np.asarray(L2_gnn_Wv).T,
        "wo": L2_gnn_Wo, "gamma": L2_gnn_gamma, "beta": L2_gnn_beta, "w1": L3_gnn_W1, "w2": L3_gnn_W2,
    }
    arrays = {f"in_{k}": np.ascontiguousarray(a) for k, a in arrays.items()}
    nc = bacc.Bacc("TRN2", target_bir_lowering=False, num_devices=1)
    args = [nc.dram_tensor(k, a.shape, mybir.dt.from_np(a.dtype), kind="ExternalInput").ap() for k, a in arrays.items()]
    result = nc.dram_tensor("out_x", x.shape, mybir.dt.from_np(np.dtype(x.dtype)), kind="ExternalOutput").ap()
    graph_layers(nc, *args, result)
    r = run_bass_kernel_spmd(nc, [arrays], core_ids=[0])
    return r.results[0]["out_x"]
```
